# Optimizing a Trainium2 kernel written in Bass

```python
import numpy as np
import jax
import jax.numpy as jnp

def _softmax(x, axis=-1):
    return jax.nn.softmax(x, axis=axis)
def _gelu(x):
    return jax.nn.gelu(x, approximate=True)
def _silu(x):
    return jax.nn.silu(x)
def _sigmoid(x):
    return jax.nn.sigmoid(x)
def _layernorm(x, axis=-1, eps=1e-5):
    m = jnp.mean(x, axis=axis, keepdims=True)
    v = jnp.var(x, axis=axis, keepdims=True)
    return (x - m) / jnp.sqrt(v + eps)
def _scatter_add(tgt, idx, src, axis=0):
    return tgt.at[idx].add(src)
def _segment_sum(src, seg, n):
    return jax.ops.segment_sum(src, seg, n)

kernel_name = 'mk_adj_resnorm_d1_adj_256_fcae62'

def setup_inputs(seed: int = 0):
    np.random.seed(seed)
    _w = jnp.asarray
    def _rec_inputs():
        import jax
        import jax.numpy as jnp
        _gk = jax.random.key(seed)
        x = -0.0002928 + 1 * jax.random.normal(jax.random.fold_in(_gk, 1), (8, 2048, 256), jnp.float32)
        _a = jax.random.bernoulli(jax.random.fold_in(_gk, 2), 0.015625, (8, 2048, 2048))
        _a = jnp.logical_or(_a, jnp.swapaxes(_a, -1, -2))
        _a = jnp.logical_or(_a, jnp.eye(2048, dtype=bool))
        adj = _a.astype(jnp.int32)
        return x, adj
    x, adj = _rec_inputs()
    def _L0_gnn_setup():
        import jax, jax.numpy as jnp
        import numpy as np
        ALPHA = 0.2
        NEG_INF = -9000000000000000.0
        key = jax.random.key(seed)
        k1, k2, k3, k4 = jax.random.split(key, 4)
        B, N, D = (8, 2048, 256)
        h = jax.random.normal(k1, (B, N, D), dtype=jnp.float32)
        adj = jax.random.randint(k2, (B, N, N), 0, 2, dtype=jnp.int32)
        W = jax.random.normal(k3, (D, D), dtype=jnp.float32) * (1.0 / np.sqrt(D))
        a = jax.random.normal(k4, (2 * D, 1), dtype=jnp.float32) * 0.05
        return {'h': h, 'adj': adj, 'W': W, 'a': a}
    _L0_gnn_all = _L0_gnn_setup()
    _L0_gnn_in = {k: v for k, v in _L0_gnn_all.items() if k in ('W', 'a', )}
    del _L0_gnn_all

    return {
        "x": x,
        "adj": adj,
        "L0_gnn_W": _L0_gnn_in["W"],
        "L0_gnn_a": _L0_gnn_in["a"],
    }

def reference(x, adj, L0_gnn_W, L0_gnn_a):
    import jax
    import jax.numpy as jnp
    def _L0_gnn_ref(h, adj, W, a):
        import jax, jax.numpy as jnp
        import numpy as np
        ALPHA = 0.2
        NEG_INF = -9000000000000000.0
        Wh = jnp.einsum('bnd,od->bno', h, W)
        D = Wh.shape[-1]
        a1, a2 = (a[:D, 0], a[D:, 0])
        s1 = Wh @ a1
        s2 = Wh @ a2
        e = jax.nn.leaky_relu(s1[:, :, None] + s2[:, None, :], negative_slope=ALPHA)
        e = jnp.where(adj > 0, e, NEG_INF)
        attention = jax.nn.softmax(e, axis=-1)
        h_prime = jnp.einsum('bij,bjd->bid', attention, Wh)
        return h_prime

    x = _layernorm(x + _L0_gnn_ref(x, adj, L0_gnn_W, L0_gnn_a), axis=-1)
    return x


_drawn_inputs = setup_inputs


def setup_inputs(seed=0):
    import zlib

    import numpy as np

    out = dict(_drawn_inputs(seed))
    spreads = {}
    factors = {}
    for name, (base, spread) in spreads.items():
        noise = np.random.default_rng([zlib.crc32(name.encode()), seed]).standard_normal(out[name].shape)
        drawn = base * np.exp(spread * noise) if base else spread * noise
        out[name] = jnp.asarray(drawn.astype(out[name].dtype))
    for name, factor in factors.items():
        out[name] = (out[name] * factor).astype(out[name].dtype)
    return out
```

```python
from contextlib import ExitStack

import concourse.bass as bass
from concourse import mybir

P = 128
ALPHA = 0.2
NEG_INF = -9.0e15
LN_EPS = 1e-5

ALU = mybir.AluOpType
ACT = mybir.ActivationFunctionType
F32 = mybir.dt.float32
I32 = mybir.dt.int32
AX_X = mybir.AxisListType.X


def gat_kernel(nc, x, adj, W, a, out):
    B, N, D = x.shape
    KB = D // P
    NT = N // P
    DE = D + 2
    TPB = 4

    xf = x.rearrange("b n d -> (b n) d")
    adjf = adj.rearrange("b n m -> (b n) m")
    outf = out.rearrange("b n d -> (b n) d")
    s2_dram = nc.dram_tensor("s2_row", [B, N], F32, kind="Internal").ap()

    with ExitStack() as ctx:
        def sb(name, shape, dt=F32):
            return ctx.enter_context(nc.sbuf_tensor(name, shape, dt))

        def psum(name, shape, dt=F32):
            return ctx.enter_context(nc.psum_tensor(name, shape, dt))

        def sem(name):
            return ctx.enter_context(nc.semaphore(name))

        ident = sb("ident", [P, P])
        w_sb = sb("w_sb", [P, KB, D])
        a_sb = sb("a_sb", [P, 2, KB])
        wt = sb("wt", [P, KB, DE])
        g_x = sb("g_x", [P, D])
        g_xT = sb("g_xT", [P, KB, P])
        g_wh = sb("g_wh", [P, NT, DE])
        g_s2 = sb("g_s2", [P, N])
        g_adj = sb("g_adj", [P, N], I32)
        g_m = sb("g_m", [P, N])
        g_e = sb("g_e", [P, N])
        g_pT = sb("g_pT", [P, NT, P])
        g_st = sb("g_st", [P, 16])
        g_xr = sb("g_xr", [P, D])
        g_y = sb("g_y", [P, D])
        g_xr2 = sb("g_xr2", [P, D])
        g_out = sb("g_out", [P, D])

        ps_a = psum("ps_a", [P, 512])
        ps_b = psum("ps_b", [P, 512])
        ps_t = psum("ps_t", [P, NT // TPB, TPB, P])

        w_in = sem("w_in")
        ident_zero = sem("ident_zero")
        ident_ok = sem("ident_ok")
        wt_ps = sem("wt_ps")
        wt_ok = sem("wt_ok")
        g_x_in = sem("g_x_in")
        g_xT_ps = sem("g_xT_ps")
        g_xT_ok = sem("g_xT_ok")
        g_wh_ps = sem("g_wh_ps")
        g_wh_ok = sem("g_wh_ok")
        g_s2_out = sem("g_s2_out")
        g_s2_in = sem("g_s2_in")
        g_adj_in = sem("g_adj_in")
        g_xr_in = sem("g_xr_in")
        g_mask_ok = sem("g_mask_ok")
        g_e_ok = sem("g_e_ok")
        g_p_ok = sem("g_p_ok")
        g_pT_ps = sem("g_pT_ps")
        g_pT_ok = sem("g_pT_ok")
        g_o_ps = sem("g_o_ps")
        g_res_ok = sem("g_res_ok")
        g_var_ok = sem("g_var_ok")
        g_std_ok = sem("g_std_ok")
        g_y_ok = sem("g_y_ok")
        g_stored = sem("g_stored")
        g_chain = sem("g_chain")

        block = ctx.enter_context(nc.Block())

        @block.sync
        def _(sp):
            sp.dma_start(w_sb[:], W.rearrange("(c p) k -> p c k", p=P)).then_inc(w_in, 16)
            with nc.allow_non_contiguous_dma("512 words once"):
                sp.dma_start(a_sb[:], a.rearrange("(h c p) one -> p h (c one)", h=2, p=P)).then_inc(w_in, 16)
            with sp.Fori(0, B) as b:
                with sp.Fori(0, NT) as t:
                    k = b * NT + t
                    sp.wait_ge(g_xT_ps, k + 1)
                    sp.dma_start(g_x[:], xf[bass.ds(k * P, P), :]).then_inc(g_x_in, 16)
                sp.wait_ge(g_wh_ok, (b + 1) * NT + 1)
                with nc.allow_non_contiguous_dma("one word of a partition and tile"):
                    sp.dma_start(s2_dram[bass.ds(b, 1), :].rearrange("o (t p) -> p (o t)", p=P),
                                 g_wh[:, :, D + 1]).then_inc(g_s2_out, 16)
                sp.wait_ge(g_s2_out, (b + 1) * 16)
                sp.dma_start(g_s2[:], s2_dram[bass.ds(b, 1), :].broadcast_to([P, N])).then_inc(g_s2_in, 16)
                with sp.Fori(0, NT) as t:
                    k = b * NT + t
                    sp.wait_ge(g_mask_ok, k + 1)
                    sp.dma_start(g_adj[:], adjf[bass.ds(k * P, P), :]).then_inc(g_adj_in, 16)
                    sp.wait_ge(g_res_ok, k + 1)
                    sp.dma_start(g_xr[:], xf[bass.ds(k * P, P), :]).then_inc(g_xr_in, 16)
                    sp.wait_ge(g_y_ok, k + 1)
                    sp.dma_start(outf[bass.ds(k * P, P), :], g_out[:]).then_inc(g_stored, 16)
            sp.wait_ge(g_stored, B * NT * 16 + 16)

        @block.gpsimd
        def _(pool):
            nc.gpsimd.memset(ident[:], 0.0).then_inc(ident_zero, 1)
            pool.wait_ge(ident_zero, 1)
            nc.gpsimd.affine_select(out=ident[:], in_=ident[:], compare_op=ALU.not_equal, fill=1.0, base=0,
                                    pattern=[[-1, P]], channel_multiplier=1).then_inc(ident_ok, 1)

        @block.tensor
        def _(pe):
            pe.wait_ge(ident_ok, 1)
            pe.wait_ge(w_in, 32)
            for kb in range(KB):
                for ob in range(KB):
                    tr = pe.transpose(ps_a[:, kb * D + ob * P:kb * D + (ob + 1) * P],
                                 w_sb[:, ob, kb * P:(kb + 1) * P], ident[:])
            tr.then_inc(g_xT_ps, 1)
            for kb in range(KB):
                for ob in range(KB):
                    mm = pe.matmul(ps_b[:, 2 * kb:2 * kb + 2], w_sb[:, ob, kb * P:(kb + 1) * P],
                                   a_sb[:, :, ob], start=(ob == 0), stop=(ob == KB - 1))
            mm.then_inc(wt_ps, 1)
            pe.wait_ge(wt_ok, 2)
            with pe.Fori(0, B) as b:
                with pe.Fori(0, NT) as t:
                    k = b * NT + t
                    pe.wait_ge(g_x_in, (k + 1) * 16)
                    for kb in range(KB):
                        mm = pe.transpose(ps_a[:, kb * P:(kb + 1) * P], g_x[:, kb * P:(kb + 1) * P], ident[:])
                    mm.then_inc(g_xT_ps, 1)
                    pe.wait_ge(g_xT_ok, k + 1)
                    pe.wait_ge(g_wh_ok, k + 1)
                    for kb in range(KB):
                        mm = pe.matmul(ps_b[:, 0:DE], g_xT[:, kb, :], wt[:, kb, :],
                                       start=(kb == 0), stop=(kb == KB - 1))
                    mm.then_inc(g_wh_ps, 1)
                with pe.Fori(0, NT) as t:
                    k = b * NT + t
                    pe.wait_ge(g_p_ok, k + 1)
                    for j in range(NT):
                        mm = pe.transpose(ps_t[:, j // TPB, j % TPB, :], g_e[:, j * P:(j + 1) * P], ident[:])
                    mm.then_inc(g_pT_ps, 1)
                    pe.wait_ge(g_pT_ok, k + 1)
                    pe.wait_ge(g_res_ok, k + 1)
                    for j in range(NT):
                        mm = pe.matmul(ps_a[:, 0:D], g_pT[:, j, :], g_wh[:, j, 0:D],
                                       start=(j == 0), stop=(j == NT - 1))
                    mm.then_inc(g_o_ps, 1)

        @block.scalar
        def _(act):
            with act.Fori(0, B * NT) as k:
                act.wait_ge(g_e_ok, k + 1)
                nc.scalar.activation(g_e[:], g_e[:], ACT.Exp, bias=g_st[:, 1:2],
                                     accum_out=g_st[:, 2:3]).then_inc(g_p_ok, 1)
                act.wait_ge(g_var_ok, k + 1)
                nc.scalar.activation(g_st[:, 12:13], g_st[:, 11:12], ACT.Sqrt).then_inc(g_std_ok, 1)

        @block.vector
        def _(dve):
            dve.wait_ge(wt_ps, 1)
            nc.vector.tensor_copy(wt[:, :, 0:D], ps_a[:, 0:KB * D].rearrange("p (k o) -> p k o", k=KB)).then_inc(wt_ok, 1)
            nc.vector.tensor_copy(wt[:, :, D:DE], ps_b[:, 0:2 * KB].rearrange("p (k o) -> p k o", k=KB)).then_inc(wt_ok, 1)
            CH = 12
            nc.vector.memset(g_st[:, 0:1], 0.0).then_inc(g_wh_ok, 1)
            nc.vector.memset(g_st[:, 1:2], 0.0).then_inc(g_mask_ok, 1)
            nc.vector.memset(g_st[:, 2:3], 0.0).then_inc(g_res_ok, 1)
            nc.vector.memset(g_st[:, 3:4], 0.0).then_inc(g_stored, 16)
            with dve.Fori(0, B) as b:
                with dve.Fori(0, NT) as t:
                    k = b * NT + t
                    dve.wait_ge(g_xT_ps, k + 2)
                    nc.vector.tensor_copy(g_xT[:], ps_a[:, 0:KB * P].rearrange("p (k o) -> p k o", k=KB)).then_inc(g_xT_ok, 1)
                    dve.wait_ge(g_wh_ps, k + 1)
                    nc.vector.tensor_copy(g_wh[:, bass.ds(t, 1), :].rearrange("p o d -> p (o d)"), ps_b[:, 0:DE]).then_inc(g_wh_ok, 1)
                with dve.Fori(0, NT) as t:
                    k = b * NT + t
                    n = [0]

                    def link(ins):
                        n[0] += 1
                        ins.then_inc(g_chain, 1)
                        dve.wait_ge(g_chain, k * CH + n[0])

                    s1 = g_wh[:, bass.ds(t, 1), D:D + 1].rearrange("p o d -> p (o d)")
                    dve.wait_ge(g_adj_in, (k + 1) * 16)
                    dve.wait_ge(g_s2_in, (b + 1) * 16)
                    nc.vector.tensor_scalar(g_m[:], g_adj[:], 0, None, ALU.is_gt).then_inc(g_mask_ok, 1)
                    link(nc.vector.tensor_scalar(g_e[:], g_s2[:], s1, None, ALU.add))
                    link(nc.vector.scalar_tensor_tensor(out=g_e[:], in0=g_e[:], scalar=ALPHA, in1=g_e[:],
                                                        op0=ALU.mult, op1=ALU.max))
                    dve.wait_ge(g_mask_ok, k + 2)
                    link(nc.vector.tensor_tensor(g_e[:], g_e[:], g_m[:], ALU.mult))
                    link(nc.vector.tensor_scalar(g_m[:], g_m[:], -1.0, -NEG_INF, ALU.add, ALU.mult))
                    link(nc.vector.tensor_tensor(g_e[:], g_e[:], g_m[:], ALU.add))
                    link(nc.vector.tensor_reduce(g_st[:, 0:1], g_e[:], AX_X, ALU.max))
                    nc.vector.tensor_scalar(g_st[:, 1:2], g_st[:, 0:1], -1.0, None, ALU.mult).then_inc(g_e_ok, 1)
                    dve.wait_ge(g_pT_ps, k + 1)
                    nc.vector.tensor_copy(g_pT[:], ps_t[:].rearrange("p b t q -> p (b t) q")).then_inc(g_pT_ok, 1)
                    dve.wait_ge(g_p_ok, k + 1)
                    link(nc.vector.reciprocal(g_st[:, 3:4], g_st[:, 2:3]))
                    dve.wait_ge(g_o_ps, k + 1)
                    dve.wait_ge(g_xr_in, (k + 1) * 16)
                    nc.vector.scalar_tensor_tensor(out=g_y[:], in0=ps_a[:, 0:D], scalar=g_st[:, 3:4], in1=g_xr[:],
                                                   op0=ALU.mult, op1=ALU.add, accum_out=g_st[:, 4:5]).then_inc(g_res_ok, 1)
                    dve.wait_ge(g_res_ok, k + 2)
                    link(nc.vector.tensor_scalar(g_st[:, 10:11], g_st[:, 4:5], 1.0 / D, None, ALU.mult))
                    link(nc.vector.tensor_scalar(g_y[:], g_y[:], g_st[:, 10:11], None, ALU.subtract))
                    link(nc.vector.scalar_tensor_tensor(out=g_xr2[:], in0=g_y[:], scalar=1.0 / D, in1=g_y[:],
                                                        op0=ALU.mult, op1=ALU.mult, accum_out=g_st[:, 5:6]))
                    nc.vector.tensor_scalar(g_st[:, 11:12], g_st[:, 5:6], LN_EPS, None, ALU.add).then_inc(g_var_ok, 1)
                    dve.wait_ge(g_std_ok, k + 1)
                    link(nc.vector.reciprocal(g_st[:, 13:14], g_st[:, 12:13]))
                    dve.wait_ge(g_stored, k * 16 + 16)
                    link(nc.vector.tensor_scalar(g_out[:], g_y[:], g_st[:, 13:14], None, ALU.mult))
                    nc.vector.tensor_copy(g_st[:, 14:15], g_out[:, 0:1]).then_inc(g_y_ok, 1)
                    assert n[0] == CH, n


_INS = ["x", "adj", "L0_gnn_W", "L0_gnn_a"]


def kernel(**inputs):
    import numpy as _np
    import concourse.bacc as _bacc
    from concourse import mybir as _mybir
    from concourse.bass_utils import run_bass_kernel_spmd as _run

    nc = _bacc.Bacc("TRN2", target_bir_lowering=False, num_devices=1)
    arrays, args = {}, []
    for name in _INS:
        arr = _np.ascontiguousarray(inputs[name])
        arrays[f"in_{name}"] = arr
        args.append(nc.dram_tensor(f"in_{name}", arr.shape, _mybir.dt.from_np(arr.dtype), kind="ExternalInput").ap())
    y = nc.dram_tensor("out_y", arrays["in_x"].shape, F32, kind="ExternalOutput").ap()
    gat_kernel(nc, *args, y)
    r = _run(nc, [arrays], core_ids=[0])
    return r.results[0]["out_y"]
```

```python
from contextlib import ExitStack

import concourse.bass as bass
from concourse import mybir

P = 128
ALPHA = 0.2
NEG_INF = -9.0e15
LN_EPS = 1e-5
SCORE_BOUND = 6.0
VAR_MIN, VAR_MAX = 1e-3, 256.0
LOG_SCALE = 2.772588722239781

ALU = mybir.AluOpType
ACT = mybir.ActivationFunctionType
F32 = mybir.dt.float32
F16 = mybir.dt.float16
F8 = mybir.dt.float8e4
I32 = mybir.dt.int32
U32 = mybir.dt.uint32
U8 = mybir.dt.uint8
AX_X = mybir.AxisListType.X

EDGE = 0x40
EDGE_WORD = 0x40404040
S2, S2A, S1, S1P, S1N, NS2 = range(6)
NE = 6
C_S1, C_NS2, C_CI, C_AI = range(4)
NC_ = 4


class Count:

    def __init__(self):
        self.base, self.n = 0, 0

    def round(self, base):
        self.base, self.n = base, 0

    def add(self, k=1):
        self.n += k
        return self.base + self.n


def gat_kernel(nc, x, adj, W, a, out):
    B, N, D = x.shape
    KB = D // P
    NT = N // P
    R = 4
    GR = R * P
    GN = N // GR
    TQ = 4
    QC = TQ * P
    DV = D + 1
    DE = D + NE
    STEPS = B * NT
    GROUPS = B * GN
    assert GN == 4 and NT == 4 * TQ and GR == 512

    xf = x.rearrange("b n d -> (b n) d")
    adjf = adj.rearrange("b n m -> (b n) m")
    outf = out.rearrange("b n d -> (b n) d")
    s1_dram = nc.dram_tensor("s1_rows", [GROUPS, GR], F32, kind="Internal").ap()

    with ExitStack() as ctx:
        def sb(name, shape, dt=F32):
            return ctx.enter_context(nc.sbuf_tensor(name, shape, dt))

        def psum(name, shape, dt=F32):
            return ctx.enter_context(nc.psum_tensor(name, shape, dt))

        def sem(name):
            return ctx.enter_context(nc.semaphore(name))

        ident = sb("ident", [P, P])
        w_sb = sb("w_sb", [P, KB, D])
        a_sb = sb("a_sb", [P, 2, KB])
        wt = sb("wt", [P, KB, DE])
        v = sb("v", [P, 2, NT, 4, D + 2], F16)
        adj_q = sb("adj_q", [P, TQ, R, QC], I32)
        mask = sb("mask", [P, N], U32)
        m1 = sb("m1", [P, 2, NT, P], U32)
        m2 = sb("m2", [P, 2, NT, P], U32)
        zb = sb("zb", [P, 2, TQ, GR], U8)
        s1r = sb("s1r", [P, 2, GR])
        xg = sb("xg", [P, 2, R, D])
        xr = sb("xr", [P, 2, R, D])
        xT = sb("xT", [P, 2, KB, P])
        yb = sb("yb", [P, 2, R, D])
        ub = sb("ub", [P, 2, DV])
        tb = sb("tb", [P, 2, DV])
        sct = sb("sct", [P, 2, 8])
        bd = sb("bd", [P, 2, 2])
        dh = sb("dh", [P, 2, 2], F16)
        scores = sb("scores", [P, STEPS, NC_])
        acg = sb("acg", [P, 2, R, 2])
        nsq = sb("nsq", [P, 2, TQ])
        rd = sb("rd", [P, 2])
        st = sb("st", [P, 2, 6])
        mv = sb("mv", [P, 2, 2])
        ve = sb("ve", [P, 2])
        rs = sb("rs", [P, 2])
        nm = sb("nm", [P, 2])
        nb = sb("nb", [P, 2])
        consts = sb("consts", [P, 4])
        ok = sb("ok", [P, 4])
        in_range = sb("in_range", [P, 2, STEPS, 2])
        verdict = sb("verdict", [P, 1], I32)
        ones = sb("ones", [P, P])
        g_st = sb("g_st", [P, 16])
        spare = sb("spare", [P, 4])

        ps_t = [psum(f"ps_t{i}", [P, 512]) for i in range(2)]
        acc1 = [psum(f"acc1_{i}", [P, 512]) for i in range(2)]
        acc2 = [psum(f"acc2_{i}", [P, 512]) for i in range(2)]
        ps_x = psum("ps_x", [P, 512])
        ps_w = psum("ps_w", [P, 512])

        w_in = sem("w_in")
        ident_zero = sem("ident_zero")
        ident_ok = sem("ident_ok")
        wt_ps = sem("wt_ps")
        wt_ok = sem("wt_ok")
        consts_ok = sem("consts_ok")
        adj_in = [sem(f"adj_in{i}") for i in range(TQ)]
        x_in = [sem(f"x_in{i}") for i in range(2)]
        xr_in = [sem(f"xr_in{i}") for i in range(2)]
        s1_out = [sem(f"s1_out{i}") for i in range(2)]
        s1_in = [sem(f"s1_in{i}") for i in range(2)]
        stored = [sem(f"stored{i}") for i in range(2)]
        mask_ok = sem("mask_ok")
        maskT_ps = sem("maskT_ps")
        m_ok = sem("m_ok")
        xT_ps = sem("xT_ps")
        xT_ok = sem("xT_ok")
        wh_ps = sem("wh_ps")
        ext_ok = sem("ext_ok")
        hi_ok = sem("hi_ok")
        lo_ok = sem("lo_ok")
        acc_ps = sem("acc_ps")
        acg_ok = sem("acg_ok")
        t_ok = sem("t_ok")
        u_ok = sem("u_ok")
        bn_ok = sem("bn_ok")
        rs_ok = sem("rs_ok")
        o_ok = sem("o_ok")
        ok_all = sem("ok_all")
        ok_all_chain = sem("ok_all_chain")
        ok_ps = sem("ok_ps")
        verdict_ok = sem("verdict_ok")
        g_x_in = sem("g_x_in")
        g_xT_ps = sem("g_xT_ps")
        g_xT_ok = sem("g_xT_ok")
        g_wh_ps = sem("g_wh_ps")
        g_wh_ok = sem("g_wh_ok")
        g_s2_out = sem("g_s2_out")
        g_s2_in = sem("g_s2_in")
        g_adj_in = sem("g_adj_in")
        g_xr_in = sem("g_xr_in")
        g_mask_ok = sem("g_mask_ok")
        g_e_ok = sem("g_e_ok")
        g_p_ok = sem("g_p_ok")
        g_pT_ps = sem("g_pT_ps")
        g_pT_ok = sem("g_pT_ok")
        g_o_ps = sem("g_o_ps")
        g_res_ok = sem("g_res_ok")
        g_var_ok = sem("g_var_ok")
        g_std_ok = sem("g_std_ok")
        g_y_ok = sem("g_y_ok")
        g_stored = sem("g_stored")
        g_chain = sem("g_chain")
        act_chain = sem("act_chain")
        dve_chain = sem("dve_chain")
        pool_chain = sem("pool_chain")
        T0, U0, A0, B0 = 2, 2, 1, 1

        g_x = xg[:, 0, 0]
        g_xT = xT[:, 0]
        g_wh = v[:, 0].rearrange("p t k d -> p (t k d)").bitcast(F32)[:, 0:NT * DE].rearrange("p (t d) -> p t d", t=NT)
        g_adj = adj_q[:, 0].rearrange("p r j -> p (r j)")
        g_s2, g_m, g_e = [adj_q[:, i].rearrange("p r j -> p (r j)").bitcast(F32) for i in (1, 2, 3)]
        g_pT = m1[:, 0].bitcast(F32)
        g_xr, g_y, g_sq, g_out = xr[:, 0, 0], yb[:, 0, 0], yb[:, 0, 1], yb[:, 1, 0]
        g_ps_t = acc1 + acc2
        g_s2_dram = s1_dram.rearrange("(b g) c -> b (g c)", b=B)

        def bank_w(at):
            return acc2[1] if at.two_banks and at.c % 2 else ps_w

        block = ctx.enter_context(nc.Block())

        class At:

            def __init__(self, b, gp, gpar, c, par):
                self.b, self.gp, self.gpar, self.c, self.par = b, gp, gpar, c, par
                self.G = b * GN + gp * 2 + gpar
                self.s = self.G * 4 + c
                last = isinstance(b, int) and isinstance(gp, int)
                G = self.G if last else 0
                self.main = not (last and self.G < 0)
                self.after_first = not last or self.s > 0
                self.two_banks = last and self.G < 0
                self.proj = not last or G + 4 < GROUPS
                self.xpose = not last or self.s + 17 < STEPS
                self.split = not last or -1 <= G < GROUPS - 1
                self.s1_out = not last or -3 <= G < GROUPS - 3
                self.mask = not last or -2 <= G < GROUPS - 2

        def wait(eng, s, value):
            if not isinstance(value, int) or value > 0:
                eng.wait_ge(s, value)

        def run(eng, group):
            for g in range(2 * GN):
                group(g // GN - 1, g % GN // 2, g % 2, 1 - g // GN)
            with eng.Fori(0, (B - 2) // 2) as pair:
                for par in (1, 0):
                    with eng.Fori(0, 2) as gp:
                        for gpar in range(2):
                            group(pair * 2 + (2 - par), gp, gpar, par)
            for g in range(GN):
                group(B - 1, g // 2, g % 2, 1)

        @block.sync
        def _(sp):
            sp.dma_start(w_sb[:], W.rearrange("(c p) k -> p c k", p=P)).then_inc(w_in, 16)
            with nc.allow_non_contiguous_dma("512 words once"):
                sp.dma_start(a_sb[:], a.rearrange("(h c p) one -> p h (c one)", h=2, p=P)).then_inc(w_in, 16)

            def known(*values):
                for value in values:
                    if not isinstance(value, int):
                        sp.compute_val(value)

            def x_rows(X):
                return xf[bass.ds(X * GR, GR), :].rearrange("(c p) d -> p c d", p=P)

            sp.dma_start(xg[:, 0], x_rows(0)).then_inc(x_in[0], 16)

            def group(b, gp, gpar, par):
                G = b * GN + gp * 2 + gpar
                static = isinstance(G, int)
                if not static or G + 5 <= GROUPS:
                    src = x_rows(min(G + 5, GROUPS - 1) if static else G + 5)
                    known(G * 4 + 16, src.offset * 4)
                    wait(sp, xT_ps, G * 4 + 16)
                    sp.dma_start(xg[:, (gpar + 1) % 2], src).then_inc(x_in[(gpar + 1) % 2], 16)
                for c in range(4):
                    if not static or -3 <= G < GROUPS - 3:
                        src = adjf[bass.ds((G + 3) * GR, GR), c * QC:(c + 1) * QC].rearrange("(p r) j -> p r j", r=R)
                        known(src.offset * 4, G * 4 + 8 + c + 1)
                        wait(sp, mask_ok, G * 4 + 8 + c + 1)
                        sp.dma_start(adj_q[:, c], src).then_inc(adj_in[c], 16)
                    if c == 1 and (not static or -1 <= G < GROUPS - 1):
                        src = x_rows(G + 1)
                        known(src.offset * 4, G * 4 + B0)
                        wait(sp, bn_ok, G * 4 + B0)
                        sp.dma_start(xr[:, (gpar + 1) % 2], src).then_inc(xr_in[(gpar + 1) % 2], 16)
                    if c == 1 and (not static or -2 <= G < GROUPS - 2):
                        src = s1_dram[bass.ds(G + 2, 1), :].broadcast_to([P, GR])
                        known(src.offset * 4, 32 * b + 16 * gp + 32, G * 4 + 4)
                        wait(sp, s1_out[gpar], 32 * b + 16 * gp + 32)
                        wait(sp, m_ok, G * 4 + 4)
                        sp.dma_start(s1r[:, gpar], src).then_inc(s1_in[gpar], 16)

            for g in range(GN):
                group(-1, g // 2, g % 2, 1)
            with sp.Fori(0, (B - 2) // 2) as pair:
                for par in range(2):
                    with sp.Fori(0, 2) as gp:
                        for gpar in range(2):
                            group(pair * 2 + par, gp, gpar, par)
            for g in range(2 * GN):
                group(B - 2 + g // GN, g % GN // 2, g % 2, g // GN)

            def general():
                with sp.Fori(0, B) as b:
                    with sp.Fori(0, NT) as t:
                        k = b * NT + t
                        rows = xf[bass.ds(k * P, P), :]
                        known(k + 1, rows.offset * 4)
                        sp.wait_ge(g_xT_ps, k + 1)
                        sp.dma_start(g_x, rows).then_inc(g_x_in, 16)
                    row = g_s2_dram[bass.ds(b, 1), :]
                    known((b + 1) * NT + 1, row.offset * 4)
                    sp.wait_ge(g_wh_ok, (b + 1) * NT + 1)
                    with nc.allow_non_contiguous_dma("one word of a partition and tile"):
                        sp.dma_start(row.rearrange("o (t p) -> p (o t)", p=P), g_wh[:, :, D + S2]).then_inc(g_s2_out, 16)
                    known((b + 1) * 16)
                    sp.wait_ge(g_s2_out, (b + 1) * 16)
                    sp.dma_start(g_s2, row.broadcast_to([P, N])).then_inc(g_s2_in, 16)
                    with sp.Fori(0, NT) as t:
                        k = b * NT + t
                        rows, arows, orows = xf[bass.ds(k * P, P), :], adjf[bass.ds(k * P, P), :], outf[bass.ds(k * P, P), :]
                        known(k + 1, rows.offset * 4, arows.offset * 4, orows.offset * 4)
                        sp.wait_ge(g_mask_ok, k + 1)
                        sp.dma_start(g_adj, arows).then_inc(g_adj_in, 16)
                        sp.wait_ge(g_res_ok, k + 1)
                        sp.dma_start(g_xr, rows).then_inc(g_xr_in, 16)
                        sp.wait_ge(g_y_ok, k + 1)
                        sp.dma_start(orows, g_out).then_inc(g_stored, 16)
                sp.wait_ge(g_stored, B * NT * 16 + 16)

            sp.wait_ge(verdict_ok, 1)
            with sp.If(sp.value_load(verdict[0:1, 0:1], min_val=0, max_val=1) != 0):
                general()

        @block.gpsimd
        def _(pool):
            nc.gpsimd.memset(ident[:], 0.0).then_inc(ident_zero, 1)
            pool.wait_ge(ident_zero, 1)
            nc.gpsimd.affine_select(out=ident[:], in_=ident[:], compare_op=ALU.not_equal, fill=1.0, base=0,
                                    pattern=[[-1, P]], channel_multiplier=1).then_inc(ident_ok, 1)
            pool.wait_ge(consts_ok, 4)
            K = 3

            def group(b, gp, gpar, par):
                for c in range(4):
                    at = At(b, gp, gpar, c, par)
                    if not at.main:
                        continue
                    i, s = c % 2, at.s
                    wait(pool, bn_ok, s + 1 + B0)
                    nc.gpsimd.tensor_tensor(ve[:, i:i + 1], mv[:, i, 1:2], consts[:, 0:1], ALU.add).then_inc(pool_chain, 1)
                    wait(pool, pool_chain, s * K + 1)
                    nc.gpsimd.tensor_tensor(rs[:, i:i + 1], ve[:, i:i + 1], consts[:, 1:2], ALU.pow).then_inc(pool_chain, 1)
                    wait(pool, pool_chain, s * K + 2)
                    nc.gpsimd.tensor_tensor(nm[:, i:i + 1], mv[:, i, 0:1], rs[:, i:i + 1], ALU.mult).then_inc(pool_chain, 1)
                    wait(pool, pool_chain, s * K + 3)
                    nc.gpsimd.tensor_tensor(nb[:, i:i + 1], consts[:, 2:3], nm[:, i:i + 1], ALU.subtract).then_inc(rs_ok, 1)

            run(pool, group)

        @block.tensor
        def _(pe):
            pe.wait_ge(ident_ok, 1)
            pe.wait_ge(w_in, 32)
            for kb in range(KB):
                for ob in range(KB):
                    mm = pe.transpose(ps_x[:, kb * D + ob * P:kb * D + (ob + 1) * P],
                                      w_sb[:, ob, kb * P:(kb + 1) * P], ident[:])
            mm.then_inc(acc_ps, A0)
            for kb in range(KB):
                for ob in range(KB):
                    mm = pe.matmul(ps_w[:, 2 * kb:2 * kb + 2], w_sb[:, ob, kb * P:(kb + 1) * P],
                                   a_sb[:, :, ob], start=(ob == 0), stop=(ob == KB - 1))
            mm.then_inc(wt_ps, 1)
            pe.wait_ge(wt_ok, 1)

            def x_tile(u):
                for kb in range(KB):
                    mm = pe.transpose(ps_x[:, kb * P:(kb + 1) * P], xg[:, u // 4, u % 4, kb * P:(kb + 1) * P], ident[:])
                mm.then_inc(xT_ps, 1)

            pe.wait_ge(x_in[0], 16)
            x_tile(0)

            def group(b, gp, gpar, par):
                for c in range(4):
                    at = At(b, gp, gpar, c, par)
                    s, G, n, m = at.s, at.G, at.s + 16, at.s + 4
                    if at.split:
                        wait(pe, mask_ok, m + 1)
                        wait(pe, m_ok, m - 1)
                        for i in range(TQ):
                            t = c * TQ + i
                            mm = pe.transpose(ps_t[c % 2][:, i * P:(i + 1) * P],
                                              mask[:].bitcast(F32)[:, t * P:(t + 1) * P], ident[:])
                        mm.then_inc(maskT_ps, 1)
                    if at.xpose or at.proj:
                        wait(pe, xT_ok, n + 1)
                    if at.xpose:
                        if c == 3:
                            wait(pe, x_in[(gpar + 1) % 2], 32 * at.b + 16 * at.gp + 16 * ((gpar + 5) // 2) + 16)
                        x_tile((gpar * 4 + c + 1) % 8)
                    if at.main:
                        if c == 0:
                            wait(pe, m_ok, G * 4 + 4)
                        if c == 0 and not at.proj:
                            wait(pe, lo_ok, at.b * NT + NT)
                        wait(pe, u_ok, s - 1 + U0)
                    if at.proj:
                        wait(pe, lo_ok, n - 1 if at.two_banks else n)
                        for kb in range(KB):
                            mm = pe.matmul(bank_w(at)[:, 0:DE], xT[:, c % 2, kb, :], wt[:, kb, :],
                                           start=(kb == 0), stop=(kb == KB - 1))
                        mm.then_inc(wh_ps, 1)
                    if at.main:
                        for t in range(NT):
                            for acc, mk, kind in ((acc1, m1, 0), (acc2, m2, 2)):
                                for lo in range(2):
                                    mm = pe.matmul(acc[c % 2][:, 0:DV],
                                                   mk[:, gpar].bitcast(F8)[:, t, c * P:(c + 1) * P],
                                                   v[:, par, t, kind + lo, 0:DV],
                                                   start=(t == 0 and lo == 0), stop=(t == NT - 1 and lo == 1))
                        mm.then_inc(acc_ps, 1)

            run(pe, group)
            pe.wait_ge(ok_all, 1)
            pe.matmul(ps_w[:, 0:1], ones[:], ok[:, 0:1], start=True, stop=True).then_inc(ok_ps, 1)

            def general():
                with pe.Fori(0, B) as b:
                    with pe.Fori(0, NT) as t:
                        k = b * NT + t
                        pe.wait_ge(g_x_in, (k + 1) * 16)
                        for kb in range(KB):
                            mm = pe.transpose(ps_x[:, kb * P:(kb + 1) * P], g_x[:, kb * P:(kb + 1) * P], ident[:])
                        mm.then_inc(g_xT_ps, 1)
                        pe.wait_ge(g_xT_ok, k + 1)
                        pe.wait_ge(g_wh_ok, k + 1)
                        for kb in range(KB):
                            mm = pe.matmul(ps_w[:, 0:DE], g_xT[:, kb, :], wt[:, kb, :],
                                           start=(kb == 0), stop=(kb == KB - 1))
                        mm.then_inc(g_wh_ps, 1)
                    with pe.Fori(0, NT) as t:
                        k = b * NT + t
                        pe.wait_ge(g_p_ok, k + 1)
                        for j in range(NT):
                            mm = pe.transpose(g_ps_t[j // TQ][:, j % TQ * P:(j % TQ + 1) * P],
                                              g_e[:, j * P:(j + 1) * P], ident[:])
                        mm.then_inc(g_pT_ps, 1)
                        pe.wait_ge(g_pT_ok, k + 1)
                        pe.wait_ge(g_res_ok, k + 1)
                        for j in range(NT):
                            mm = pe.matmul(ps_x[:, 0:D], g_pT[:, j, :], g_wh[:, j, 0:D],
                                           start=(j == 0), stop=(j == NT - 1))
                        mm.then_inc(g_o_ps, 1)

            pe.wait_ge(verdict_ok, 1)
            with pe.If(pe.value_load(verdict[0:1, 0:1], min_val=0, max_val=1) != 0):
                general()

        @block.scalar
        def _(act):
            act.wait_ge(consts_ok, 4)
            act.wait_ge(wt_ps, 1)
            nc.scalar.activation(wt[:, :, 0:D], ps_x[:, 0:KB * D].rearrange("p (k o) -> p k o", k=KB), ACT.Copy)
            sc12 = ps_w[:, 0:2 * KB].rearrange("p (k o) -> p k o", k=KB)
            for col, h, f in ((S2, 1, 1.0), (S2A, 1, ALPHA), (S1, 0, 1.0), (S1P, 0, 1 - ALPHA),
                              (S1N, 0, ALPHA - 1), (NS2, 1, -1.0)):
                last = nc.scalar.activation(wt[:, :, D + col:D + col + 1], sc12[:, :, h:h + 1], ACT.Copy, scale=f)
            last.then_inc(wt_ok, 1)
            nc.scalar.activation(spare[:, 0:1], consts[:, 0:1], ACT.Copy).then_inc(t_ok, T0)
            act.wait_ge(xT_ps, 1)
            nc.scalar.activation(xT[:, 0], ps_x[:, 0:KB * P].rearrange("p (k o) -> p k o", k=KB), ACT.Copy)\
              .then_inc(xT_ok, 1)
            K = 2

            def normalise(at, back=1):
                last = at.c - back
                slot, c = (at.gpar, last) if last >= 0 else (1 - at.gpar, 3)
                group = at.G if last >= 0 else at.G - 1
                k = at.s - back + 1
                wait(act, rs_ok, k)
                nc.scalar.activation(yb[:, slot, c], yb[:, slot, c], ACT.Identity,
                                     bias=nb[:, c % 2:c % 2 + 1], scale=rs[:, c % 2:c % 2 + 1]).then_inc(o_ok, 1)
                if c == 3:
                    wait(act, o_ok, k)
                    act.dma_start(outf[bass.ds(group * GR, GR), :].rearrange("(c p) d -> p c d", p=P),
                                  yb[:, slot]).then_inc(stored[slot], 16)

            def group(b, gp, gpar, par):
                for c in range(4):
                    at = At(b, gp, gpar, c, par)
                    s, n, i = at.s, at.s + 16, c % 2
                    t = at.gp * 8 + gpar * 4 + c
                    bank = bank_w(at)
                    if at.xpose:
                        wait(act, xT_ps, n + 2)
                        wait(act, wh_ps, n)
                        nc.scalar.activation(xT[:, 1 - i], ps_x[:, 0:KB * P].rearrange("p (k o) -> p k o", k=KB),
                                             ACT.Copy).then_inc(xT_ok, 1)
                    if c == 1 and at.s1_out:
                        wait(act, lo_ok, at.G * 4 + 16)
                        wait(act, s1_in[1 - gpar], 32 * at.b + 16 * at.gp + 16 * ((gpar + 1) // 2) + 16)
                        with nc.allow_non_contiguous_dma("512 words"):
                            act.dma_start(s1_dram[bass.ds(at.G + 3, 1), :].rearrange("o (c p) -> p (o c)", p=P),
                                          scores[:, bass.ds(at.G * 4 + 12, 4), C_S1]).then_inc(s1_out[1 - gpar], 16)
                    if at.proj:
                        wait(act, wh_ps, n + 1)
                        wait(act, lo_ok, n - 1)
                        nc.scalar.activation(sct[:, i, 0:1], bank[:, D + S1:D + S1 + 1], ACT.Copy)
                        nc.scalar.activation(sct[:, i, 1:2], bank[:, D + NS2:D + NS2 + 1], ACT.Copy)
                        nc.scalar.activation(sct[:, i, 4:6], bank[:, D + S1P:D + S1N + 1], ACT.Relu).then_inc(act_chain, 1)
                        nc.scalar.activation(bd[:, i], bank[:, D + S2:D + S2A + 1], ACT.Exp,
                                             bias=consts[:, 3:4]).then_inc(act_chain, 1)
                        wait(act, act_chain, n * K + 1)
                        nc.scalar.activation(sct[:, i, 2:4], sct[:, i, 4:6], ACT.Exp, scale=-1.0).then_inc(ext_ok, 1)
                        wait(act, act_chain, n * K + 2)
                        nc.scalar.activation(dh[:, i], bd[:, i], ACT.Copy)
                        for h in range(2):
                            hi = nc.scalar.activation(
                                v[:, 1 - par, bass.ds(t, 1), 2 * h, 0:D].rearrange("p o d -> p (o d)"),
                                bank[:, 0:D], ACT.Identity, scale=bd[:, i, h:h + 1])
                        hi.then_inc(hi_ok, 1)
                    if at.main:
                        if at.after_first:
                            normalise(at)
                        if c == 0:
                            wait(act, acg_ok, at.G + 1)
                        wait(act, acc_ps, s + 1 + A0)
                        wait(act, u_ok, s - 1 + U0)
                        nc.scalar.activation(tb[:, i], acc2[i][:, 0:DV], ACT.Identity,
                                             scale=acg[:, gpar, c, 0:1]).then_inc(t_ok, 1)

            run(act, group)
            normalise(At(B - 1, 1, 1, 3, 1), back=0)
            for i in range(2):
                act.wait_ge(stored[i], GROUPS // 2 * 16 + 16)

            def general():
                with act.Fori(0, B * NT) as k:
                    act.wait_ge(g_e_ok, k + 1)
                    nc.scalar.activation(g_e, g_e, ACT.Exp, bias=g_st[:, 1:2],
                                         accum_out=g_st[:, 2:3]).then_inc(g_p_ok, 1)
                    act.wait_ge(g_var_ok, k + 1)
                    nc.scalar.activation(g_st[:, 12:13], g_st[:, 11:12], ACT.Sqrt).then_inc(g_std_ok, 1)

            act.wait_ge(verdict_ok, 1)
            with act.If(act.value_load(verdict[0:1, 0:1], min_val=0, max_val=1) != 0):
                general()

        @block.vector
        def _(dve):
            nc.vector.memset(consts[:, 0:1], LN_EPS).then_inc(consts_ok, 1)
            nc.vector.memset(consts[:, 1:2], -0.5).then_inc(consts_ok, 1)
            nc.vector.memset(consts[:, 2:3], 0.0).then_inc(consts_ok, 1)
            nc.vector.memset(consts[:, 3:4], LOG_SCALE).then_inc(consts_ok, 1)
            nc.vector.memset(ok[:], 1.0).then_inc(stored[0], 16)
            nc.vector.memset(mv[:], 1.0).then_inc(bn_ok, B0)
            nc.vector.memset(spare[:, 1:2], 0.0).then_inc(stored[1], 16)
            nc.vector.memset(spare[:, 2:3], 0.0).then_inc(u_ok, U0)
            chain = Count()

            def link(ins):
                ins.then_inc(dve_chain, 1)
                chain.add()

            def linked():
                dve.wait_ge(dve_chain, chain.base + chain.n)

            def check(i, k):
                wait(dve, bn_ok, k)
                nc.vector.scalar_tensor_tensor(out=ok[:, 0:1], in0=mv[:, i, 1:2], scalar=VAR_MIN, in1=ok[:, 0:1],
                                               op0=ALU.is_gt, op1=ALU.mult)
                nc.vector.scalar_tensor_tensor(out=ok[:, 1:2], in0=mv[:, i, 1:2], scalar=VAR_MAX, in1=ok[:, 1:2],
                                               op0=ALU.is_lt, op1=ALU.mult)

            per_group = 4 * 7
            seen = {}

            def group(b, gp, gpar, par):
                static = isinstance(b, int) and isinstance(gp, int)
                G = b * GN + gp * 2 + gpar
                if not static:
                    chain.round(seen["start"] + G * per_group)
                elif G == GROUPS - GN:
                    chain.round(seen["start"] + G * per_group)
                for c in range(4):
                    at = At(b, gp, gpar, c, par)
                    s, n, m, i = at.s, at.s + 16, at.s + 4, c % 2
                    t = at.gp * 8 + gpar * 4 + c
                    if at.main:
                        check(1 - i, s + B0)
                    if at.mask:
                        wait(dve, maskT_ps, m + 1)
                        wait(dve, adj_in[c], (at.G + 3) * 16)
                        nc.vector.tensor_scalar(
                            mask[:].bitcast(U8)[:, c * QC * R:(c + 1) * QC * R].rearrange("p (j r) -> p r j", r=R),
                            adj_q[:, c], 0, float(EDGE - 1), ALU.is_gt, ALU.add).then_inc(mask_ok, 1)
                    if at.proj:
                        wait(dve, ext_ok, n + 1)
                        link(nc.vector.tensor_scalar(scores[:, bass.ds(n, 1), :].rearrange("p o d -> p (o d)"),
                                                     sct[:, i, 0:NC_], 1.0, None, ALU.mult))
                    if at.split:
                        tile0 = (at.b + (at.gp if gpar else 0)) * NT if not static else (at.G + 1) // GN * NT
                        if at.proj:
                            linked()
                        link(nc.vector.tensor_scalar(nsq[:, i], scores[:, bass.ds(tile0 + c * TQ, TQ), C_NS2],
                                                     1.0, None, ALU.mult))
                        if c == 0:
                            wait(dve, s1_in[1 - gpar], 32 * at.b + 16 * at.gp + 16 * ((gpar + 1) // 2) + 16)
                        linked()
                        for j in range(TQ):
                            z = nc.vector.tensor_scalar(zb[:, i, j], s1r[:, 1 - gpar], nsq[:, i, j:j + 1],
                                                        float(EDGE), ALU.is_gt, ALU.mult)
                        link(z)
                        if not at.mask:
                            wait(dve, maskT_ps, m + 1)
                        if c == 0:
                            wait(dve, acc_ps, s + A0)
                        linked()
                        w1 = m1[:, 1 - gpar, c * TQ:(c + 1) * TQ].rearrange("p t q -> p (t q)")
                        w2 = m2[:, 1 - gpar, c * TQ:(c + 1) * TQ].rearrange("p t q -> p (t q)")
                        link(nc.vector.tensor_tensor(w1, ps_t[i][:].bitcast(U32),
                                                     zb[:, i].rearrange("p t q -> p (t q)").bitcast(U32),
                                                     ALU.bitwise_and))
                        linked()
                        nc.vector.scalar_tensor_tensor(out=w2, in0=ps_t[i][:].bitcast(U32), scalar=EDGE_WORD, in1=w1,
                                                       op0=ALU.bitwise_and, op1=ALU.bitwise_xor).then_inc(m_ok, 1)
                    if at.proj:
                        wait(dve, hi_ok, n + 1)
                        vt = v[:, 1 - par, bass.ds(t, 1), :, :].rearrange("p o k d -> p (o k) d")
                        for h in range(2):
                            nc.vector.scalar_tensor_tensor(out=vt[:, 2 * h + 1, 0:D], in0=bank_w(at)[:, 0:D],
                                                           scalar=bd[:, i, h:h + 1], in1=vt[:, 2 * h, 0:D],
                                                           op0=ALU.mult, op1=ALU.subtract)
                        nc.vector.tensor_scalar(vt[:, 0:4:2, D], dh[:, i], 1.0, None, ALU.mult)
                        nc.vector.tensor_tensor(vt[:, 1:4:2, D], bd[:, i], dh[:, i], ALU.subtract).then_inc(lo_ok, 1)
                    if at.main:
                        if c == 0:
                            nc.vector.tensor_scalar(acg[:, gpar], scores[:, bass.ds(at.G * 4, 4), C_CI:C_AI + 1],
                                                    1.0, None, ALU.mult).then_inc(acg_ok, 1)
                            wait(dve, acg_ok, at.G + 1)
                        wait(dve, acc_ps, s + 1 + A0)
                        wait(dve, t_ok, s + 1 + T0)
                        nc.vector.scalar_tensor_tensor(out=ub[:, i], in0=acc1[i][:, 0:DV], scalar=acg[:, gpar, c, 1:2],
                                                       in1=tb[:, i], op0=ALU.mult, op1=ALU.add).then_inc(u_ok, 1)
                        wait(dve, u_ok, s + 1 + U0)
                        link(nc.vector.reciprocal(rd[:, i:i + 1], ub[:, i, D:DV]))
                        if c == 0:
                            wait(dve, xr_in[gpar], 32 * at.b + 16 * at.gp + 16)
                            wait(dve, stored[gpar], 32 * at.b + 16 * at.gp + 16)
                        linked()
                        link(nc.vector.scalar_tensor_tensor(out=yb[:, gpar, c], in0=ub[:, i, 0:D],
                                                            scalar=rd[:, i:i + 1], in1=xr[:, gpar, c],
                                                            op0=ALU.mult, op1=ALU.add))
                        linked()
                        link(nc.vector.bn_stats(st[:, i], yb[:, gpar, c]))
                        linked()
                        nc.vector.memset(spare[:, 3:4], 0.0)
                        nc.vector.bn_aggr(mv[:, i], st[:, i]).then_inc(bn_ok, 1)
                if static and G == -1:
                    seen["start"] = chain.base + chain.n

            run(dve, group)
            check(1, STEPS + B0)
            flat = [in_range[:, i].rearrange("p s c -> p (s c)") for i in range(2)]
            nc.vector.memset(ones[:], 1.0).then_inc(ok_all_chain, 1)
            nc.vector.tensor_scalar(in_range[:, 0], scores[:, :, C_S1:C_NS2 + 1], SCORE_BOUND, None, ALU.is_lt)\
              .then_inc(ok_all_chain, 1)
            dve.wait_ge(ok_all_chain, 2)
            nc.vector.scalar_tensor_tensor(out=in_range[:, 1], in0=scores[:, :, C_S1:C_NS2 + 1], scalar=-SCORE_BOUND,
                                           in1=in_range[:, 0], op0=ALU.is_gt, op1=ALU.mult).then_inc(ok_all_chain, 1)
            dve.wait_ge(ok_all_chain, 3)
            nc.vector.tensor_reduce(ok[:, 2:3], flat[1], AX_X, ALU.min).then_inc(ok_all_chain, 1)
            nc.vector.tensor_tensor(ok[:, 3:4], ok[:, 0:1], ok[:, 1:2], ALU.mult).then_inc(ok_all_chain, 1)
            dve.wait_ge(ok_all_chain, 5)
            nc.vector.tensor_tensor(ok[:, 0:1], ok[:, 2:3], ok[:, 3:4], ALU.mult).then_inc(ok_all, 1)
            for i in range(2):
                dve.wait_ge(stored[i], GROUPS // 2 * 16 + 16)
            dve.wait_ge(ok_ps, 1)
            nc.vector.tensor_scalar(verdict[:], ps_w[:, 0:1], P - 0.5, None, ALU.is_lt).then_inc(verdict_ok, 1)

            def general():
                CH = 11
                for i, free in enumerate((g_xT_ps, g_wh_ok, g_mask_ok, g_res_ok)):
                    nc.vector.memset(g_st[:, i:i + 1], 0.0).then_inc(free, 1)
                nc.vector.memset(g_st[:, 4:5], 0.0).then_inc(g_stored, 16)
                with dve.Fori(0, B) as b:
                    with dve.Fori(0, NT) as t:
                        k = b * NT + t
                        dve.wait_ge(g_xT_ps, k + 2)
                        nc.vector.tensor_copy(g_xT, ps_x[:, 0:KB * P].rearrange("p (k o) -> p k o", k=KB))\
                          .then_inc(g_xT_ok, 1)
                        dve.wait_ge(g_wh_ps, k + 1)
                        nc.vector.tensor_copy(g_wh[:, bass.ds(t, 1), :].rearrange("p o d -> p (o d)"), ps_w[:, 0:DE])\
                          .then_inc(g_wh_ok, 1)
                    with dve.Fori(0, NT) as t:
                        k = b * NT + t
                        n = [0]

                        def link(ins):
                            n[0] += 1
                            ins.then_inc(g_chain, 1)
                            dve.wait_ge(g_chain, k * CH + n[0])

                        s1 = g_wh[:, bass.ds(t, 1), D + S1:D + S1 + 1].rearrange("p o d -> p (o d)")
                        dve.wait_ge(g_adj_in, (k + 1) * 16)
                        dve.wait_ge(g_s2_in, (b + 1) * 16)
                        nc.vector.tensor_scalar(g_m, g_adj, 0, None, ALU.is_gt).then_inc(g_mask_ok, 1)
                        link(nc.vector.tensor_scalar(g_e, g_s2, s1, None, ALU.add))
                        link(nc.vector.scalar_tensor_tensor(out=g_e, in0=g_e, scalar=ALPHA, in1=g_e,
                                                            op0=ALU.mult, op1=ALU.max))
                        dve.wait_ge(g_mask_ok, k + 2)
                        link(nc.vector.tensor_tensor(g_e, g_e, g_m, ALU.mult))
                        link(nc.vector.tensor_scalar(g_m, g_m, -1.0, -NEG_INF, ALU.add, ALU.mult))
                        link(nc.vector.tensor_tensor(g_e, g_e, g_m, ALU.add))
                        link(nc.vector.tensor_reduce(g_st[:, 0:1], g_e, AX_X, ALU.max))
                        nc.vector.tensor_scalar(g_st[:, 1:2], g_st[:, 0:1], -1.0, None, ALU.mult).then_inc(g_e_ok, 1)
                        dve.wait_ge(g_pT_ps, k + 1)
                        for j in range(NT // TQ):
                            cp = nc.vector.tensor_copy(g_pT[:, j * TQ:(j + 1) * TQ].rearrange("p t q -> p (t q)"),
                                                       g_ps_t[j][:])
                        cp.then_inc(g_pT_ok, 1)
                        dve.wait_ge(g_p_ok, k + 1)
                        link(nc.vector.reciprocal(g_st[:, 3:4], g_st[:, 2:3]))
                        dve.wait_ge(g_o_ps, k + 1)
                        dve.wait_ge(g_xr_in, (k + 1) * 16)
                        nc.vector.scalar_tensor_tensor(out=g_y, in0=ps_x[:, 0:D], scalar=g_st[:, 3:4], in1=g_xr,
                                                       op0=ALU.mult, op1=ALU.add, accum_out=g_st[:, 4:5])\
                          .then_inc(g_res_ok, 1)
                        dve.wait_ge(g_res_ok, k + 2)
                        link(nc.vector.tensor_scalar(g_st[:, 10:11], g_st[:, 4:5], 1.0 / D, None, ALU.mult))
                        link(nc.vector.tensor_scalar(g_y, g_y, g_st[:, 10:11], None, ALU.subtract))
                        link(nc.vector.scalar_tensor_tensor(out=g_sq, in0=g_y, scalar=1.0 / D, in1=g_y,
                                                            op0=ALU.mult, op1=ALU.mult, accum_out=g_st[:, 5:6]))
                        nc.vector.tensor_scalar(g_st[:, 11:12], g_st[:, 5:6], LN_EPS, None, ALU.add).then_inc(g_var_ok, 1)
                        dve.wait_ge(g_std_ok, k + 1)
                        link(nc.vector.reciprocal(g_st[:, 13:14], g_st[:, 12:13]))
                        dve.wait_ge(g_stored, k * 16 + 16)
                        nc.vector.tensor_scalar(g_out, g_y, g_st[:, 13:14], None, ALU.mult).then_inc(g_y_ok, 1)
                        assert n[0] == CH, n

            dve.wait_ge(verdict_ok, 1)
            with dve.If(dve.value_load(verdict[0:1, 0:1], min_val=0, max_val=1) != 0):
                general()


_INS = ["x", "adj", "L0_gnn_W", "L0_gnn_a"]


def kernel(**inputs):
    import numpy as _np
    import concourse.bacc as _bacc
    from concourse import mybir as _mybir
    from concourse.bass_utils import run_bass_kernel_spmd as _run

    nc = _bacc.Bacc("TRN2", target_bir_lowering=False, num_devices=1)
    arrays, args = {}, []
    for name in _INS:
        arr = _np.ascontiguousarray(inputs[name])
        arrays[f"in_{name}"] = arr
        args.append(nc.dram_tensor(f"in_{name}", arr.shape, _mybir.dt.from_np(arr.dtype), kind="ExternalInput").ap())
    y = nc.dram_tensor("out_y", arrays["in_x"].shape, F32, kind="ExternalOutput").ap()
    gat_kernel(nc, *args, y)
    r = _run(nc, [arrays], core_ids=[0])
    return r.results[0]["out_y"]
```

```python
import math
from contextlib import ExitStack

import concourse.bass as bass
from concourse import mybir

P = 128
ALPHA = 0.2
NEG_INF = -9.0e15
LN_EPS = 1e-5
SCORE_BOUND = 6.0
VAR_MIN, VAR_MAX = 1e-3, 256.0
XW_SCALE = 64.0
WH_SCALE = XW_SCALE * XW_SCALE
BD_SCALE = 16.0
LOG_SCALE = math.log(BD_SCALE / WH_SCALE)

ALU = mybir.AluOpType
ACT = mybir.ActivationFunctionType
F32 = mybir.dt.float32
F16 = mybir.dt.float16
F8 = mybir.dt.float8e4
I32 = mybir.dt.int32
U32 = mybir.dt.uint32
U8 = mybir.dt.uint8
AX_X = mybir.AxisListType.X

EDGE = 0x40
EDGE_WORD = 0x40404040
S2, S2A, S1, NS2, S1P, S1N = range(6)
NE = 6
C_S1, C_NS2, C_CI, C_AI = range(4)
NC_ = 4


class Count:

    def __init__(self):
        self.base, self.n = 0, 0

    def round(self, base):
        self.base, self.n = base, 0

    def add(self, k=1):
        self.n += k
        return self.base + self.n


def gat_kernel(nc, x, adj, W, a, out):
    B, N, D = x.shape
    KB = D // P
    NT = N // P
    R = 4
    GR = R * P
    GN = N // GR
    TQ = 4
    QC = TQ * P
    DV = D + 1
    DE = D + NE
    STEPS = B * NT
    GROUPS = B * GN
    assert GN == 4 and NT == 4 * TQ and GR == 512

    xf = x.rearrange("b n d -> (b n) d")
    adjf = adj.rearrange("b n m -> (b n) m")
    outf = out.rearrange("b n d -> (b n) d")
    s1_dram = nc.dram_tensor("s1_rows", [GROUPS, GR], F32, kind="Internal").ap()

    with ExitStack() as ctx:
        def sb(name, shape, dt=F32):
            return ctx.enter_context(nc.sbuf_tensor(name, shape, dt))

        def psum(name, shape, dt=F32):
            return ctx.enter_context(nc.psum_tensor(name, shape, dt))

        def sem(name):
            return ctx.enter_context(nc.semaphore(name))

        ident = sb("ident", [P, P])
        w_sb = sb("w_sb", [P, KB, D])
        a_sb = sb("a_sb", [P, 2, KB])
        wt = sb("wt", [P, KB, DE])
        v = sb("v", [P, 2, NT, 4, D + 2], F16)
        adj_q = sb("adj_q", [P, TQ, R, QC], I32)
        mask = sb("mask", [P, N], U32)
        m1 = sb("m1", [P, 2, NT, P], U32)
        m2 = sb("m2", [P, 2, NT, P], U32)
        zb = sb("zb", [P, 2, TQ, GR], U8)
        s1r = sb("s1r", [P, 2, GR])
        xg = sb("xg", [P, 2, R, D])
        xr = sb("xr", [P, 2, R, D])
        wt_hl = sb("wt_hl", [P, 2, KB, DE], F16)
        xT = sb("xT", [P, 2, 2, KB, P], F16)
        yb = sb("yb", [P, 2, R, D])
        ub = sb("ub", [P, 2, DV])
        tb = sb("tb", [P, 2, DV])
        rl = sb("rl", [P, 2, 2])
        bd = sb("bd", [P, 2, 2])
        dh = sb("dh", [P, 2, 2], F16)
        scores = sb("scores", [P, STEPS, NC_])
        acg = sb("acg", [P, 2, R, 2])
        nsq = sb("nsq", [P, 2, TQ])
        rd = sb("rd", [P, 2])
        st = sb("st", [P, 2, 6])
        mv = sb("mv", [P, 2, R, 2])
        ve = sb("ve", [P, 2])
        rs = sb("rs", [P, 2])
        nm = sb("nm", [P, 2])
        nb = sb("nb", [P, 2])
        consts = sb("consts", [P, 4])
        ok = sb("ok", [P, 2, R])
        all_ok = sb("all_ok", [P, 4])
        in_range = sb("in_range", [P, 2, STEPS, 2])
        verdict = sb("verdict", [P, 1], I32)
        ones = sb("ones", [P, P])
        g_st = sb("g_st", [P, 16])
        spare = sb("spare", [P, 4])

        ps_t = [psum(f"ps_t{i}", [P, 512]) for i in range(2)]
        acc1 = [psum(f"acc1_{i}", [P, 512]) for i in range(2)]
        acc2 = [psum(f"acc2_{i}", [P, 512]) for i in range(2)]
        ps_x = psum("ps_x", [P, 512])
        ps_w = psum("ps_w", [P, 512])

        w_in = sem("w_in")
        ident_zero = sem("ident_zero")
        ident_ok = sem("ident_ok")
        wt_ps = sem("wt_ps")
        wt_ok = sem("wt_ok")
        consts_ok = sem("consts_ok")
        adj_in = [sem(f"adj_in{i}") for i in range(TQ)]
        x_in = [sem(f"x_in{i}") for i in range(2)]
        xr_in = [sem(f"xr_in{i}") for i in range(2)]
        s1_out = [sem(f"s1_out{i}") for i in range(2)]
        s1_in = [sem(f"s1_in{i}") for i in range(2)]
        stored = [sem(f"stored{i}") for i in range(2)]
        mask_ok = sem("mask_ok")
        maskT_ps = sem("maskT_ps")
        m_ok = sem("m_ok")
        xT_ps = sem("xT_ps")
        xT_hi_ok = sem("xT_hi_ok")
        xT_ok = sem("xT_ok")
        wt_hi_ok = sem("wt_hi_ok")
        wt_lo_ok = sem("wt_lo_ok")
        wh_ps = sem("wh_ps")
        ext_ok = sem("ext_ok")
        hi_ok = sem("hi_ok")
        lo_ok = sem("lo_ok")
        acc_ps = sem("acc_ps")
        acg_ok = sem("acg_ok")
        t_ok = sem("t_ok")
        u_ok = sem("u_ok")
        bn_ok = sem("bn_ok")
        rs_ok = sem("rs_ok")
        o_ok = sem("o_ok")
        ok_all = sem("ok_all")
        ok_all_chain = sem("ok_all_chain")
        ok_ps = sem("ok_ps")
        verdict_ok = sem("verdict_ok")
        g_x_in = sem("g_x_in")
        g_xT_ps = sem("g_xT_ps")
        g_xT_ok = sem("g_xT_ok")
        g_wh_ps = sem("g_wh_ps")
        g_wh_ok = sem("g_wh_ok")
        g_s2_out = sem("g_s2_out")
        g_s2_in = sem("g_s2_in")
        g_adj_in = sem("g_adj_in")
        g_xr_in = sem("g_xr_in")
        g_mask_ok = sem("g_mask_ok")
        g_e_ok = sem("g_e_ok")
        g_p_ok = sem("g_p_ok")
        g_pT_ps = sem("g_pT_ps")
        g_pT_ok = sem("g_pT_ok")
        g_o_ps = sem("g_o_ps")
        g_res_ok = sem("g_res_ok")
        g_var_ok = sem("g_var_ok")
        g_std_ok = sem("g_std_ok")
        g_y_ok = sem("g_y_ok")
        g_stored = sem("g_stored")
        g_chain = sem("g_chain")
        act_chain = sem("act_chain")
        dve_chain = sem("dve_chain")
        pool_chain = sem("pool_chain")
        T0, U0, A0, B0 = 2, 2, 1, 1

        g_x = xg[:, 0, 0]
        g_xT = ub[:, 0, 0:KB * P].rearrange("p (k n) -> p k n", k=KB)
        g_wh = v[:, 0].rearrange("p t k d -> p (t k d)").bitcast(F32)[:, 0:NT * DE].rearrange("p (t d) -> p t d", t=NT)
        g_adj = adj_q[:, 0].rearrange("p r j -> p (r j)")
        g_s2, g_m, g_e = [adj_q[:, i].rearrange("p r j -> p (r j)").bitcast(F32) for i in (1, 2, 3)]
        g_pT = m1[:, 0].bitcast(F32)
        g_xr, g_y, g_sq, g_out = xr[:, 0, 0], yb[:, 0, 0], yb[:, 0, 1], yb[:, 1, 0]
        g_ps_t = acc1 + acc2
        g_s2_dram = s1_dram.rearrange("(b g) c -> b (g c)", b=B)

        def bank_w(at):
            return acc2[1] if at.two_banks and at.c % 2 else ps_w

        block = ctx.enter_context(nc.Block())

        class At:

            def __init__(self, b, gp, gpar, c, par):
                self.b, self.gp, self.gpar, self.c, self.par = b, gp, gpar, c, par
                self.G = b * GN + gp * 2 + gpar
                self.s = self.G * 4 + c
                last = isinstance(b, int) and isinstance(gp, int)
                G = self.G if last else 0
                self.main = not (last and self.G < 0)
                self.after_first = not last or self.s > 0
                self.two_banks = last and self.G < 0
                self.proj = not last or G + 4 < GROUPS
                self.xpose = not last or self.s + 17 < STEPS
                self.split = not last or -1 <= G < GROUPS - 1
                self.s1_out = not last or -3 <= G < GROUPS - 3
                self.first_masks = last and self.G == -3
                self.mask = not last or TQ <= self.s + 5 < STEPS

        def wait(eng, s, value):
            if not isinstance(value, int) or value > 0:
                eng.wait_ge(s, value)

        def run(eng, group):
            for g in range(2 * GN):
                group(g // GN - 1, g % GN // 2, g % 2, 1 - g // GN)
            with eng.Fori(0, (B - 2) // 2) as pair:
                for par in (1, 0):
                    with eng.Fori(0, 2) as gp:
                        for gpar in range(2):
                            group(pair * 2 + (2 - par), gp, gpar, par)
            for g in range(GN):
                group(B - 1, g // 2, g % 2, 1)

        @block.sync
        def _(sp):
            sp.dma_start(w_sb[:], W.rearrange("(c p) k -> p c k", p=P)).then_inc(w_in, 16)
            with nc.allow_non_contiguous_dma("512 words once"):
                sp.dma_start(a_sb[:], a.rearrange("(h c p) one -> p h (c one)", h=2, p=P)).then_inc(w_in, 16)

            def known(*values):
                for value in values:
                    if not isinstance(value, int):
                        sp.compute_val(value)

            def x_rows(X):
                return xf[bass.ds(X * GR, GR), :].rearrange("(c p) d -> p c d", p=P)

            def load_quad(X, c, masks):
                src = adjf[bass.ds(X * GR, GR), c * QC:(c + 1) * QC].rearrange("(p r) j -> p r j", r=R)
                known(src.offset * 4, masks)
                wait(sp, mask_ok, masks)
                sp.dma_start(adj_q[:, c], src).then_inc(adj_in[c], 16)

            sp.dma_start(xg[:, 0], x_rows(0)).then_inc(x_in[0], 16)
            sp.dma_start(xg[:, 1], x_rows(1)).then_inc(x_in[1], 16)
            for c in range(4):
                load_quad(0, c, 0)

            def group(b, gp, gpar, par):
                G = b * GN + gp * 2 + gpar
                static = isinstance(G, int)
                if not static or -2 <= G < GROUPS - 2:
                    src = s1_dram[bass.ds(G + 2, 1), :].broadcast_to([P, GR])
                    known(src.offset * 4, 32 * b + 16 * gp + 32, G * 4 + 4)
                    wait(sp, s1_out[gpar], 32 * b + 16 * gp + 32)
                    wait(sp, m_ok, G * 4 + 4)
                    sp.dma_start(s1r[:, gpar], src).then_inc(s1_in[gpar], 16)
                if not static or -GN < G <= GROUPS - 5:
                    src = x_rows(min(G + 5, GROUPS - 1) if static else G + 5)
                    known(G * 4 + 16, src.offset * 4)
                    wait(sp, xT_ps, G * 4 + 16)
                    sp.dma_start(xg[:, (gpar + 1) % 2], src).then_inc(x_in[(gpar + 1) % 2], 16)
                for c in range(4):
                    if not static or -1 <= G < GROUPS - 2:
                        load_quad(G + 2, c, G * 4 + 4 + c + 1)
                    if c == 1 and (not static or -1 <= G < GROUPS - 1):
                        src = x_rows(G + 1)
                        known(src.offset * 4, G * 4 + B0)
                        wait(sp, bn_ok, G * 4 + B0)
                        sp.dma_start(xr[:, (gpar + 1) % 2], src).then_inc(xr_in[(gpar + 1) % 2], 16)

            for g in range(GN):
                group(-1, g // 2, g % 2, 1)
            with sp.Fori(0, (B - 2) // 2) as pair:
                for par in range(2):
                    with sp.Fori(0, 2) as gp:
                        for gpar in range(2):
                            group(pair * 2 + par, gp, gpar, par)
            for g in range(2 * GN):
                group(B - 2 + g // GN, g % GN // 2, g % 2, g // GN)

            def general():
                with sp.Fori(0, B) as b:
                    with sp.Fori(0, NT) as t:
                        k = b * NT + t
                        rows = xf[bass.ds(k * P, P), :]
                        known(k + 1, rows.offset * 4)
                        sp.wait_ge(g_xT_ps, k + 1)
                        sp.dma_start(g_x, rows).then_inc(g_x_in, 16)
                    row = g_s2_dram[bass.ds(b, 1), :]
                    known((b + 1) * NT + 1, row.offset * 4)
                    sp.wait_ge(g_wh_ok, (b + 1) * NT + 1)
                    with nc.allow_non_contiguous_dma("one word of a partition and tile"):
                        sp.dma_start(row.rearrange("o (t p) -> p (o t)", p=P), g_wh[:, :, D + S2]).then_inc(g_s2_out, 16)
                    known((b + 1) * 16)
                    sp.wait_ge(g_s2_out, (b + 1) * 16)
                    sp.dma_start(g_s2, row.broadcast_to([P, N])).then_inc(g_s2_in, 16)
                    with sp.Fori(0, NT) as t:
                        k = b * NT + t
                        rows, arows, orows = xf[bass.ds(k * P, P), :], adjf[bass.ds(k * P, P), :], outf[bass.ds(k * P, P), :]
                        known(k + 1, rows.offset * 4, arows.offset * 4, orows.offset * 4)
                        sp.wait_ge(g_mask_ok, k + 1)
                        sp.dma_start(g_adj, arows).then_inc(g_adj_in, 16)
                        sp.wait_ge(g_res_ok, k + 1)
                        sp.dma_start(g_xr, rows).then_inc(g_xr_in, 16)
                        sp.wait_ge(g_y_ok, k + 1)
                        sp.dma_start(orows, g_out).then_inc(g_stored, 16)
                sp.wait_ge(g_stored, B * NT * 16 + 16)

            sp.wait_ge(verdict_ok, 1)
            with sp.If(sp.value_load(verdict[0:1, 0:1], min_val=0, max_val=1) != 0):
                general()

        @block.gpsimd
        def _(pool):
            nc.gpsimd.memset(ident[:], 0.0).then_inc(ident_zero, 1)
            pool.wait_ge(ident_zero, 1)
            nc.gpsimd.affine_select(out=ident[:], in_=ident[:], compare_op=ALU.not_equal, fill=1.0, base=0,
                                    pattern=[[-1, P]], channel_multiplier=1).then_inc(ident_ok, 1)
            pool.wait_ge(consts_ok, 4)
            K = 3

            def group(b, gp, gpar, par):
                for c in range(4):
                    at = At(b, gp, gpar, c, par)
                    if not at.main:
                        continue
                    i, s = c % 2, at.s
                    wait(pool, bn_ok, s + 1 + B0)
                    nc.gpsimd.tensor_tensor(ve[:, i:i + 1], mv[:, gpar, c, 1:2], consts[:, 0:1], ALU.add).then_inc(pool_chain, 1)
                    wait(pool, pool_chain, s * K + 1)
                    nc.gpsimd.tensor_tensor(rs[:, i:i + 1], ve[:, i:i + 1], consts[:, 1:2], ALU.pow).then_inc(pool_chain, 1)
                    wait(pool, pool_chain, s * K + 2)
                    nc.gpsimd.tensor_tensor(nm[:, i:i + 1], mv[:, gpar, c, 0:1], rs[:, i:i + 1], ALU.mult).then_inc(pool_chain, 1)
                    wait(pool, pool_chain, s * K + 3)
                    nc.gpsimd.tensor_tensor(nb[:, i:i + 1], consts[:, 2:3], nm[:, i:i + 1], ALU.subtract).then_inc(rs_ok, 1)

            run(pool, group)

        @block.tensor
        def _(pe):
            pe.wait_ge(ident_ok, 1)
            pe.wait_ge(w_in, 32)
            for kb in range(KB):
                for ob in range(KB):
                    mm = pe.transpose(acc1[0][:, kb * D + ob * P:kb * D + (ob + 1) * P],
                                      w_sb[:, ob, kb * P:(kb + 1) * P], ident[:])
            mm.then_inc(acc_ps, A0)
            for kb in range(KB):
                for ob in range(KB):
                    mm = pe.matmul(acc1[1][:, 2 * kb:2 * kb + 2], w_sb[:, ob, kb * P:(kb + 1) * P],
                                   a_sb[:, :, ob], start=(ob == 0), stop=(ob == KB - 1))
            mm.then_inc(wt_ps, 1)

            PARTS = ((0, 0), (1, 0), (0, 1))

            def x_tile(u):
                for kb in range(KB):
                    mm = pe.transpose(ps_x[:, kb * P:(kb + 1) * P], xg[:, u // 4, u % 4, kb * P:(kb + 1) * P], ident[:])
                mm.then_inc(xT_ps, 1)

            pe.wait_ge(x_in[0], 16)
            x_tile(0)
            pe.wait_ge(wt_lo_ok, 1)

            def group(b, gp, gpar, par):
                for c in range(4):
                    at = At(b, gp, gpar, c, par)
                    s, G, n, m = at.s, at.G, at.s + 16, at.s + 4
                    if at.split:
                        wait(pe, mask_ok, m + 1)
                        wait(pe, m_ok, m - 1)
                        for i in range(TQ):
                            t = c * TQ + i
                            mm = pe.transpose(ps_t[c % 2][:, i * P:(i + 1) * P],
                                              mask[:].bitcast(F32)[:, t * P:(t + 1) * P], ident[:])
                        mm.then_inc(maskT_ps, 1)
                    if at.xpose or at.proj:
                        wait(pe, xT_ok, n + 1)
                    if at.xpose:
                        if c == 3:
                            wait(pe, x_in[(gpar + 1) % 2], 32 * at.b + 16 * at.gp + 16 * ((gpar + 5) // 2) + 16)
                        x_tile((gpar * 4 + c + 1) % 8)
                    if at.main:
                        if c == 0:
                            wait(pe, m_ok, G * 4 + 4)
                        if c == 0 and not at.proj:
                            wait(pe, lo_ok, at.b * NT + NT)
                        wait(pe, u_ok, s - 1 + U0)
                    if at.proj:
                        wait(pe, lo_ok, n - 1 if at.two_banks else n)
                        for kb in range(KB):
                            for xp, wp in PARTS:
                                mm = pe.matmul(bank_w(at)[:, 0:DE], xT[:, c % 2, xp, kb, :], wt_hl[:, wp, kb, :],
                                               start=(kb == 0 and xp + wp == 0), stop=(kb == KB - 1 and wp == 1))
                        mm.then_inc(wh_ps, 1)
                    if at.main:
                        for t in range(NT):
                            for acc, mk, kind in ((acc1, m1, 0), (acc2, m2, 2)):
                                for lo in range(2):
                                    mm = pe.matmul(acc[c % 2][:, 0:DV],
                                                   mk[:, gpar].bitcast(F8)[:, t, c * P:(c + 1) * P],
                                                   v[:, par, t, kind + lo, 0:DV],
                                                   start=(t == 0 and lo == 0), stop=(t == NT - 1 and lo == 1))
                        mm.then_inc(acc_ps, 1)

            run(pe, group)
            pe.wait_ge(ok_all, 1)
            pe.matmul(ps_w[:, 0:1], ones[:], all_ok[:, 2:3], start=True, stop=True).then_inc(ok_ps, 1)

            def general():
                with pe.Fori(0, B) as b:
                    with pe.Fori(0, NT) as t:
                        k = b * NT + t
                        pe.wait_ge(g_x_in, (k + 1) * 16)
                        for kb in range(KB):
                            mm = pe.transpose(ps_x[:, kb * P:(kb + 1) * P], g_x[:, kb * P:(kb + 1) * P], ident[:])
                        mm.then_inc(g_xT_ps, 1)
                        pe.wait_ge(g_xT_ok, k + 1)
                        pe.wait_ge(g_wh_ok, k + 1)
                        for kb in range(KB):
                            mm = pe.matmul(ps_w[:, 0:DE], g_xT[:, kb, :], wt[:, kb, :],
                                           start=(kb == 0), stop=(kb == KB - 1))
                        mm.then_inc(g_wh_ps, 1)
                    with pe.Fori(0, NT) as t:
                        k = b * NT + t
                        pe.wait_ge(g_p_ok, k + 1)
                        for j in range(NT):
                            mm = pe.transpose(g_ps_t[j // TQ][:, j % TQ * P:(j % TQ + 1) * P],
                                              g_e[:, j * P:(j + 1) * P], ident[:])
                        mm.then_inc(g_pT_ps, 1)
                        pe.wait_ge(g_pT_ok, k + 1)
                        pe.wait_ge(g_res_ok, k + 1)
                        for j in range(NT):
                            mm = pe.matmul(ps_x[:, 0:D], g_pT[:, j, :], g_wh[:, j, 0:D],
                                           start=(j == 0), stop=(j == NT - 1))
                        mm.then_inc(g_o_ps, 1)

            pe.wait_ge(verdict_ok, 1)
            with pe.If(pe.value_load(verdict[0:1, 0:1], min_val=0, max_val=1) != 0):
                general()

        @block.scalar
        def _(act):
            act.wait_ge(consts_ok, 4)
            nc.scalar.activation(spare[:, 0:1], consts[:, 0:1], ACT.Exp).then_inc(t_ok, T0)
            act.wait_ge(wt_ps, 1)
            nc.scalar.activation(wt[:, :, 0:D], acc1[0][:, 0:KB * D].rearrange("p (k o) -> p k o", k=KB), ACT.Copy)
            sc12 = acc1[1][:, 0:2 * KB].rearrange("p (k o) -> p k o", k=KB)
            for col, h, f in ((S2, 1, 1.0), (S2A, 1, ALPHA), (S1, 0, 1.0), (S1P, 0, 1 - ALPHA),
                              (S1N, 0, ALPHA - 1), (NS2, 1, -1.0)):
                last = nc.scalar.activation(wt[:, :, D + col:D + col + 1], sc12[:, :, h:h + 1], ACT.Copy, scale=f)
            last.then_inc(wt_ok, 1)
            act.wait_ge(xT_ps, 1)
            nc.scalar.activation(xT[:, 0, 0], ps_x[:, 0:KB * P].rearrange("p (k o) -> p k o", k=KB), ACT.Copy,
                                 scale=XW_SCALE)\
              .then_inc(xT_hi_ok, 1)
            act.wait_ge(wt_ok, 1)
            nc.scalar.activation(wt_hl[:, 0], wt[:], ACT.Copy, scale=XW_SCALE).then_inc(wt_hi_ok, 1)
            K = 2

            def normalise(at, back=1):
                last = at.c - back
                slot, c = (at.gpar, last) if last >= 0 else (1 - at.gpar, 3)
                group = at.G if last >= 0 else at.G - 1
                k = at.s - back + 1
                wait(act, rs_ok, k)
                nc.scalar.activation(yb[:, slot, c], yb[:, slot, c], ACT.Identity,
                                     bias=nb[:, c % 2:c % 2 + 1], scale=rs[:, c % 2:c % 2 + 1]).then_inc(o_ok, 1)
                if c == 3:
                    wait(act, o_ok, k)
                    act.dma_start(outf[bass.ds(group * GR, GR), :].rearrange("(c p) d -> p c d", p=P),
                                  yb[:, slot]).then_inc(stored[slot], 16)

            def group(b, gp, gpar, par):
                for c in range(4):
                    at = At(b, gp, gpar, c, par)
                    s, n, i = at.s, at.s + 16, c % 2
                    t = at.gp * 8 + gpar * 4 + c
                    bank = bank_w(at)
                    if at.xpose:
                        wait(act, xT_ps, n + 2)
                        wait(act, wh_ps, n)
                        nc.scalar.activation(xT[:, 1 - i, 0], ps_x[:, 0:KB * P].rearrange("p (k o) -> p k o", k=KB),
                                             ACT.Copy, scale=XW_SCALE).then_inc(xT_hi_ok, 1)
                    if c == 1 and at.s1_out:
                        wait(act, ext_ok, at.G * 4 + 16)
                        wait(act, s1_in[1 - gpar], 32 * at.b + 16 * at.gp + 16 * ((gpar + 1) // 2) + 16)
                        with nc.allow_non_contiguous_dma("512 words"):
                            act.dma_start(s1_dram[bass.ds(at.G + 3, 1), :].rearrange("o (c p) -> p (o c)", p=P),
                                          scores[:, bass.ds(at.G * 4 + 12, 4), C_S1]).then_inc(s1_out[1 - gpar], 16)
                    if at.proj:
                        wait(act, wh_ps, n + 1)
                        wait(act, lo_ok, n - 1)
                        nc.scalar.activation(rl[:, i], bank[:, D + S1P:D + S1N + 1], ACT.Relu,
                                             scale=1 / WH_SCALE).then_inc(act_chain, 1)
                        wait(act, act_chain, n * K + 1)
                        nc.scalar.activation(bd[:, i], bank[:, D + S2:D + S2A + 1], ACT.Exp,
                                             scale=1 / WH_SCALE, bias=consts[:, 3:4]).then_inc(act_chain, 1)
                        row = scores[:, bass.ds(n, 1), :].rearrange("p o d -> p (o d)")
                        nc.scalar.activation(row[:, C_S1:C_NS2 + 1], bank[:, D + S1:D + NS2 + 1], ACT.Copy,
                                             scale=1 / WH_SCALE)
                        nc.scalar.activation(row[:, C_CI:C_AI + 1], rl[:, i], ACT.Exp, scale=-1.0).then_inc(ext_ok, 1)
                        wait(act, act_chain, n * K + 2)
                        nc.scalar.activation(dh[:, i], bd[:, i], ACT.Copy, scale=WH_SCALE)
                        vt = v[:, 1 - par, bass.ds(t, 1), :, :].rearrange("p o k d -> p (o k) d")
                        nc.scalar.activation(vt[:, 0:4:2, D], bd[:, i], ACT.Copy, scale=WH_SCALE)
                        for h in range(2):
                            hi = nc.scalar.activation(vt[:, 2 * h, 0:D], bank[:, 0:D], ACT.Identity,
                                                      scale=bd[:, i, h:h + 1])
                        hi.then_inc(hi_ok, 1)
                    if at.main:
                        if at.after_first:
                            normalise(at)
                        if c == 0:
                            wait(act, acg_ok, at.G + 1)
                        wait(act, acc_ps, s + 1 + A0)
                        wait(act, u_ok, s - 1 + U0)
                        nc.scalar.activation(tb[:, i], acc2[i][:, 0:DV], ACT.Identity,
                                             scale=acg[:, gpar, c, 0:1]).then_inc(t_ok, 1)

            run(act, group)
            normalise(At(B - 1, 1, 1, 3, 1), back=0)
            for i in range(2):
                act.wait_ge(stored[i], GROUPS // 2 * 16 + 16)

            def general():
                with act.Fori(0, B * NT) as k:
                    act.wait_ge(g_e_ok, k + 1)
                    nc.scalar.activation(g_e, g_e, ACT.Exp, bias=g_st[:, 1:2],
                                         accum_out=g_st[:, 2:3]).then_inc(g_p_ok, 1)
                    act.wait_ge(g_var_ok, k + 1)
                    nc.scalar.activation(g_st[:, 12:13], g_st[:, 11:12], ACT.Sqrt).then_inc(g_std_ok, 1)

            act.wait_ge(verdict_ok, 1)
            with act.If(act.value_load(verdict[0:1, 0:1], min_val=0, max_val=1) != 0):
                general()

        @block.vector
        def _(dve):
            nc.vector.memset(consts[:, 0:1], LN_EPS).then_inc(consts_ok, 1)
            nc.vector.memset(consts[:, 1:2], -0.5).then_inc(consts_ok, 1)
            nc.vector.memset(consts[:, 2:3], 0.0).then_inc(consts_ok, 1)
            nc.vector.memset(consts[:, 3:4], LOG_SCALE).then_inc(consts_ok, 1)
            nc.vector.memset(ok[:], 1.0).then_inc(stored[0], 16)
            nc.vector.memset(mv[:], 1.0).then_inc(bn_ok, B0)
            nc.vector.memset(spare[:, 1:2], 0.0).then_inc(stored[1], 16)
            nc.vector.memset(spare[:, 2:3], 0.0).then_inc(u_ok, U0)
            chain = Count()

            def link(ins):
                ins.then_inc(dve_chain, 1)
                return chain.add()

            def x_low(i, k):
                wait(dve, xT_hi_ok, k + 1)
                nc.vector.scalar_tensor_tensor(out=xT[:, i, 1],
                                               in0=ps_x[:, 0:KB * P].rearrange("p (k o) -> p k o", k=KB),
                                               scalar=XW_SCALE, in1=xT[:, i, 0],
                                               op0=ALU.mult, op1=ALU.subtract).then_inc(xT_ok, 1)

            x_low(0, 0)
            dve.wait_ge(wt_hi_ok, 1)
            nc.vector.scalar_tensor_tensor(out=wt_hl[:, 1], in0=wt[:], scalar=XW_SCALE, in1=wt_hl[:, 0],
                                           op0=ALU.mult, op1=ALU.subtract).then_inc(wt_lo_ok, 1)

            class Finish:

                def __init__(self, at, back=1):
                    last = at.c - back
                    self.on = at.after_first and at.main
                    self.slot, self.c = (at.gpar, last) if last >= 0 else (1 - at.gpar, 3)
                    self.at, self.k, self.i = at, at.s - back + 1, self.c % 2

                def sums(self):
                    i, at = self.i, self.at
                    if self.c == 0:
                        wait(dve, acg_ok, at.G + 1)
                    wait(dve, acc_ps, self.k + A0)
                    wait(dve, t_ok, self.k + T0)
                    nc.vector.scalar_tensor_tensor(out=ub[:, i], in0=acc1[i][:, 0:DV],
                                                   scalar=acg[:, self.slot, self.c, 1:2],
                                                   in1=tb[:, i], op0=ALU.mult, op1=ALU.add).then_inc(u_ok, 1)

                def divisor(self):
                    i = self.i
                    wait(dve, u_ok, self.k + U0)
                    self.rd = link(nc.vector.reciprocal(rd[:, i:i + 1], ub[:, i, D:DV]))

                def residual(self):
                    i, at = self.i, self.at
                    if self.c == 0:
                        wait(dve, xr_in[self.slot], 32 * at.b + 16 * at.gp + 16)
                        wait(dve, stored[self.slot], 32 * at.b + 16 * at.gp + 16)
                    wait(dve, dve_chain, self.rd)
                    self.y = link(nc.vector.scalar_tensor_tensor(out=yb[:, self.slot, self.c], in0=ub[:, i, 0:D],
                                                                 scalar=rd[:, i:i + 1], in1=xr[:, self.slot, self.c],
                                                                 op0=ALU.mult, op1=ALU.add))

                def moments(self):
                    wait(dve, dve_chain, self.y)
                    self.st = link(nc.vector.bn_stats(st[:, self.i], yb[:, self.slot, self.c]))

                def variance(self):
                    wait(dve, dve_chain, self.st)
                    nc.vector.memset(spare[:, 3:4], 0.0)
                    nc.vector.bn_aggr(mv[:, self.slot, self.c], st[:, self.i]).then_inc(bn_ok, 1)

                def check(self):
                    if self.c < 3:
                        return
                    wait(dve, bn_ok, self.k + B0)
                    var = mv[:, self.slot, :, 1]
                    nc.vector.scalar_tensor_tensor(out=ok[:, 0], in0=var, scalar=VAR_MIN, in1=ok[:, 0],
                                                   op0=ALU.is_gt, op1=ALU.mult)
                    nc.vector.scalar_tensor_tensor(out=ok[:, 1], in0=var, scalar=VAR_MAX, in1=ok[:, 1],
                                                   op0=ALU.is_lt, op1=ALU.mult)

            per_group = 4 * 6
            seen = {}

            def group(b, gp, gpar, par):
                static = isinstance(b, int) and isinstance(gp, int)
                G = b * GN + gp * 2 + gpar
                if not static or G == GROUPS - GN:
                    chain.round(seen["start"] + (G - GN) * per_group)
                for c in range(4):
                    at = At(b, gp, gpar, c, par)
                    s, n, m, i = at.s, at.s + 16, at.s + 4, c % 2
                    t = at.gp * 8 + gpar * 4 + c
                    rows = Finish(at)
                    if at.main and c == 0:
                        nc.vector.tensor_scalar(acg[:, gpar], scores[:, bass.ds(at.G * 4, 4), C_CI:C_AI + 1],
                                                1.0, None, ALU.mult).then_inc(acg_ok, 1)
                    if at.xpose and not rows.on:
                        x_low(1 - i, n + 1)
                    if at.mask or at.first_masks:
                        slot, group_of = (c, 0) if at.first_masks else ((c + 1) % TQ, at.G + (c + 5) // TQ)
                        wait(dve, adj_in[slot], (group_of + 1) * 16)
                        nc.vector.tensor_scalar(
                            mask[:].bitcast(U8)[:, slot * QC * R:(slot + 1) * QC * R].rearrange("p (j r) -> p r j", r=R),
                            adj_q[:, slot], 0, float(EDGE - 1), ALU.is_gt, ALU.add).then_inc(mask_ok, 1)
                    if rows.on:
                        rows.sums()
                    if at.xpose and rows.on:
                        x_low(1 - i, n + 1)
                    if rows.on:
                        rows.divisor()
                    if rows.on:
                        rows.residual()
                    if rows.on:
                        rows.moments()
                    if at.split:
                        tile0 = (at.b + (at.gp if gpar else 0)) * NT if not static else (at.G + 1) // GN * NT
                        if at.proj:
                            wait(dve, ext_ok, n + 1)
                        quad = link(nc.vector.tensor_scalar(nsq[:, i], scores[:, bass.ds(tile0 + c * TQ, TQ), C_NS2],
                                                            1.0, None, ALU.mult))
                    if rows.on:
                        rows.variance()
                    if at.split:
                        if c == 0:
                            wait(dve, s1_in[1 - gpar], 32 * at.b + 16 * at.gp + 16 * ((gpar + 1) // 2) + 16)
                        wait(dve, dve_chain, quad)
                        for j in range(TQ):
                            z = nc.vector.tensor_scalar(zb[:, i, j], s1r[:, 1 - gpar], nsq[:, i, j:j + 1],
                                                        float(EDGE), ALU.is_gt, ALU.mult)
                        signs = link(z)
                    if rows.on:
                        rows.check()
                    vt = v[:, 1 - par, bass.ds(t, 1), :, :].rearrange("p o k d -> p (o k) d")

                    def low(h):
                        return nc.vector.scalar_tensor_tensor(out=vt[:, 2 * h + 1, 0:D], in0=bank_w(at)[:, 0:D],
                                                              scalar=bd[:, i, h:h + 1], in1=vt[:, 2 * h, 0:D],
                                                              op0=ALU.mult, op1=ALU.subtract)

                    if at.split:
                        wait(dve, maskT_ps, m + 1)
                        wait(dve, dve_chain, signs)
                        w1 = m1[:, 1 - gpar, c * TQ:(c + 1) * TQ].rearrange("p t q -> p (t q)")
                        w2 = m2[:, 1 - gpar, c * TQ:(c + 1) * TQ].rearrange("p t q -> p (t q)")
                        positive = link(nc.vector.tensor_tensor(w1, ps_t[i][:].bitcast(U32),
                                                                zb[:, i].rearrange("p t q -> p (t q)").bitcast(U32),
                                                                ALU.bitwise_and))
                    if at.proj:
                        wait(dve, hi_ok, n + 1)
                        low(0)
                    if at.split:
                        wait(dve, dve_chain, positive)
                        nc.vector.scalar_tensor_tensor(out=w2, in0=ps_t[i][:].bitcast(U32), scalar=EDGE_WORD, in1=w1,
                                                       op0=ALU.bitwise_and, op1=ALU.bitwise_xor).then_inc(m_ok, 1)
                    if at.proj:
                        low(1)
                        nc.vector.scalar_tensor_tensor(out=vt[:, 1:4:2, D], in0=bd[:, i], scalar=WH_SCALE, in1=dh[:, i],
                                                       op0=ALU.mult, op1=ALU.subtract).then_inc(lo_ok, 1)
                if static and G == GN - 1:
                    seen["start"] = chain.base + chain.n

            run(dve, group)
            rows = Finish(At(B - 1, 1, 1, 3, 1), back=0)
            rows.sums()
            rows.divisor()
            rows.residual()
            rows.moments()
            rows.variance()
            rows.check()
            flat = [in_range[:, i].rearrange("p s c -> p (s c)") for i in range(2)]
            nc.vector.memset(ones[:], 1.0).then_inc(ok_all_chain, 1)
            nc.vector.tensor_scalar(in_range[:, 0], scores[:, :, C_S1:C_NS2 + 1], SCORE_BOUND, None, ALU.is_lt)\
              .then_inc(ok_all_chain, 1)
            dve.wait_ge(ok_all_chain, 2)
            nc.vector.scalar_tensor_tensor(out=in_range[:, 1], in0=scores[:, :, C_S1:C_NS2 + 1], scalar=-SCORE_BOUND,
                                           in1=in_range[:, 0], op0=ALU.is_gt, op1=ALU.mult).then_inc(ok_all_chain, 1)
            dve.wait_ge(ok_all_chain, 3)
            nc.vector.tensor_reduce(all_ok[:, 0:1], flat[1], AX_X, ALU.min).then_inc(ok_all_chain, 1)
            nc.vector.tensor_reduce(all_ok[:, 1:2], ok[:].rearrange("p k r -> p (k r)"), AX_X, ALU.min)\
              .then_inc(ok_all_chain, 1)
            dve.wait_ge(ok_all_chain, 5)
            nc.vector.tensor_tensor(all_ok[:, 2:3], all_ok[:, 0:1], all_ok[:, 1:2], ALU.mult).then_inc(ok_all, 1)
            dve.wait_ge(ok_ps, 1)
            nc.vector.tensor_scalar(verdict[:], ps_w[:, 0:1], P - 0.5, None, ALU.is_lt).then_inc(verdict_ok, 1)

            def general():
                CH = 11
                for i in range(2):
                    dve.wait_ge(stored[i], GROUPS // 2 * 16 + 16)
                for i, free in enumerate((g_xT_ps, g_wh_ok, g_mask_ok, g_res_ok)):
                    nc.vector.memset(g_st[:, i:i + 1], 0.0).then_inc(free, 1)
                nc.vector.memset(g_st[:, 4:5], 0.0).then_inc(g_stored, 16)
                with dve.Fori(0, B) as b:
                    with dve.Fori(0, NT) as t:
                        k = b * NT + t
                        dve.wait_ge(g_xT_ps, k + 2)
                        nc.vector.tensor_copy(g_xT, ps_x[:, 0:KB * P].rearrange("p (k o) -> p k o", k=KB))\
                          .then_inc(g_xT_ok, 1)
                        dve.wait_ge(g_wh_ps, k + 1)
                        nc.vector.tensor_copy(g_wh[:, bass.ds(t, 1), :].rearrange("p o d -> p (o d)"), ps_w[:, 0:DE])\
                          .then_inc(g_wh_ok, 1)
                    with dve.Fori(0, NT) as t:
                        k = b * NT + t
                        n = [0]

                        def link(ins):
                            n[0] += 1
                            ins.then_inc(g_chain, 1)
                            dve.wait_ge(g_chain, k * CH + n[0])

                        s1 = g_wh[:, bass.ds(t, 1), D + S1:D + S1 + 1].rearrange("p o d -> p (o d)")
                        dve.wait_ge(g_adj_in, (k + 1) * 16)
                        dve.wait_ge(g_s2_in, (b + 1) * 16)
                        nc.vector.tensor_scalar(g_m, g_adj, 0, None, ALU.is_gt).then_inc(g_mask_ok, 1)
                        link(nc.vector.tensor_scalar(g_e, g_s2, s1, None, ALU.add))
                        link(nc.vector.scalar_tensor_tensor(out=g_e, in0=g_e, scalar=ALPHA, in1=g_e,
                                                            op0=ALU.mult, op1=ALU.max))
                        dve.wait_ge(g_mask_ok, k + 2)
                        link(nc.vector.tensor_tensor(g_e, g_e, g_m, ALU.mult))
                        link(nc.vector.tensor_scalar(g_m, g_m, -1.0, -NEG_INF, ALU.add, ALU.mult))
                        link(nc.vector.tensor_tensor(g_e, g_e, g_m, ALU.add))
                        link(nc.vector.tensor_reduce(g_st[:, 0:1], g_e, AX_X, ALU.max))
                        nc.vector.tensor_scalar(g_st[:, 1:2], g_st[:, 0:1], -1.0, None, ALU.mult).then_inc(g_e_ok, 1)
                        dve.wait_ge(g_pT_ps, k + 1)
                        for j in range(NT // TQ):
                            cp = nc.vector.tensor_copy(g_pT[:, j * TQ:(j + 1) * TQ].rearrange("p t q -> p (t q)"),
                                                       g_ps_t[j][:])
                        cp.then_inc(g_pT_ok, 1)
                        dve.wait_ge(g_p_ok, k + 1)
                        link(nc.vector.reciprocal(g_st[:, 3:4], g_st[:, 2:3]))
                        dve.wait_ge(g_o_ps, k + 1)
                        dve.wait_ge(g_xr_in, (k + 1) * 16)
                        nc.vector.scalar_tensor_tensor(out=g_y, in0=ps_x[:, 0:D], scalar=g_st[:, 3:4], in1=g_xr,
                                                       op0=ALU.mult, op1=ALU.add, accum_out=g_st[:, 4:5])\
                          .then_inc(g_res_ok, 1)
                        dve.wait_ge(g_res_ok, k + 2)
                        link(nc.vector.tensor_scalar(g_st[:, 10:11], g_st[:, 4:5], 1.0 / D, None, ALU.mult))
                        link(nc.vector.tensor_scalar(g_y, g_y, g_st[:, 10:11], None, ALU.subtract))
                        link(nc.vector.scalar_tensor_tensor(out=g_sq, in0=g_y, scalar=1.0 / D, in1=g_y,
                                                            op0=ALU.mult, op1=ALU.mult, accum_out=g_st[:, 5:6]))
                        nc.vector.tensor_scalar(g_st[:, 11:12], g_st[:, 5:6], LN_EPS, None, ALU.add).then_inc(g_var_ok, 1)
                        dve.wait_ge(g_std_ok, k + 1)
                        link(nc.vector.reciprocal(g_st[:, 13:14], g_st[:, 12:13]))
                        dve.wait_ge(g_stored, k * 16 + 16)
                        nc.vector.tensor_scalar(g_out, g_y, g_st[:, 13:14], None, ALU.mult).then_inc(g_y_ok, 1)
                        assert n[0] == CH, n

            dve.wait_ge(verdict_ok, 1)
            with dve.If(dve.value_load(verdict[0:1, 0:1], min_val=0, max_val=1) != 0):
                general()


_INS = ["x", "adj", "L0_gnn_W", "L0_gnn_a"]


def kernel(**inputs):
    import numpy as _np
    import concourse.bacc as _bacc
    from concourse import mybir as _mybir
    from concourse.bass_utils import run_bass_kernel_spmd as _run

    nc = _bacc.Bacc("TRN2", target_bir_lowering=False, num_devices=1)
    arrays, args = {}, []
    for name in _INS:
        arr = _np.ascontiguousarray(inputs[name])
        arrays[f"in_{name}"] = arr
        args.append(nc.dram_tensor(f"in_{name}", arr.shape, _mybir.dt.from_np(arr.dtype), kind="ExternalInput").ap())
    y = nc.dram_tensor("out_y", arrays["in_x"].shape, F32, kind="ExternalOutput").ap()
    gat_kernel(nc, *args, y)
    r = _run(nc, [arrays], core_ids=[0])
    return r.results[0]["out_y"]
```
